# Optimizing a Trainium2 kernel written in Bass

```python
import numpy as np
import jax
import jax.numpy as jnp

def _softmax(x, axis=-1):
    return jax.nn.softmax(x, axis=axis)

def _gelu(x):
    return jax.nn.gelu(x, approximate=True)

def _silu(x):
    return jax.nn.silu(x)

def _sigmoid(x):
    return jax.nn.sigmoid(x)

def _layernorm(x, axis=-1, eps=1e-05):
    m = jnp.mean(x, axis=axis, keepdims=True)
    v = jnp.var(x, axis=axis, keepdims=True)
    return (x - m) / jnp.sqrt(v + eps)

def _scatter_add(tgt, idx, src, axis=0):
    return tgt.at[idx].add(src)

def _segment_sum(src, seg, n):
    return jax.ops.segment_sum(src, seg, n)
kernel_name = 'mk_sandwich_d2_jaxref_r8_bfc744'

def setup_inputs(seed: int=0):
    np.random.seed(seed)
    _w = jnp.asarray

    def _L0_attn_setup():
        import jax, jax.numpy as jnp
        import numpy as np
        DIM = 128
        HEADS = 16
        HEAD_DIM = DIM // HEADS
        B, S = (4, 512)
        key = jax.random.key(seed)
        ks = jax.random.split(key, 8)
        sc = 1.0 / np.sqrt(DIM)
        return {'x': jax.random.normal(ks[0], (B, S, DIM), dtype=jnp.float32), 'Wq': jax.random.normal(ks[1], (DIM, DIM), dtype=jnp.float32) * sc, 'Wk': jax.random.normal(ks[2], (DIM, DIM), dtype=jnp.float32) * sc, 'Wv': jax.random.normal(ks[3], (DIM, DIM), dtype=jnp.float32) * sc, 'Wp': jax.random.normal(ks[4], (DIM, DIM), dtype=jnp.float32) * sc, 'bp': jnp.zeros((DIM,), dtype=jnp.float32), 'conv_w': jax.random.normal(ks[5], (DIM, 3), dtype=jnp.float32) * (1.0 / np.sqrt(3.0)), 'conv_b': jnp.zeros((DIM,), dtype=jnp.float32)}
    _L0_attn_in = _L0_attn_setup()

    def _L0_ffn_setup():
        import jax, jax.numpy as jnp
        import numpy as np
        DIM = 128
        DEPTH = 6
        HEADS = 16
        DIM_HEAD = 64
        WINDOW = 32
        INNER = HEADS * DIM_HEAD
        DIM_INNER = int(DIM * 4 * 2 / 3)
        QK_SCALE = 8.0

        def shift_tokens(t):
            a, s = jnp.split(t, 2, -1)
            s = jnp.pad(s, ((0, 0), (1, 0), (0, 0)))[:, :-1]
            return jnp.concatenate([a, s], -1)

        def l2norm(t):
            return t / jnp.maximum(jnp.linalg.norm(t, axis=-1, keepdims=True), 1e-12)

        def rotate_half(x):
            x1, x2 = jnp.split(x, 2, -1)
            return jnp.concatenate([-x2, x1], -1)

        def rotary_tables(n):
            half = jnp.arange(0, DIM_HEAD, 2, dtype=jnp.float32)
            inv_freq = 1.0 / 10000.0 ** (half / DIM_HEAD)
            t = jnp.arange(n, dtype=jnp.float32)
            freqs = t[:, None] * inv_freq[None, :]
            freqs = jnp.concatenate([freqs, freqs], -1)
            base_scale = (half + 0.4 * DIM_HEAD) / (1.4 * DIM_HEAD)
            power = (t - n // 2) / (WINDOW // 2)
            scale = base_scale[None, :] ** power[:, None]
            scale = jnp.concatenate([scale, scale], -1)
            return (freqs, scale)

        def local_attention(q, k, v):
            b, h, n, d = q.shape
            w = WINDOW
            nw = n // w
            bq = q.reshape(b, h, nw, w, d)
            bk = k.reshape(b, h, nw, w, d)
            bv = v.reshape(b, h, nw, w, d)

            def look(t):
                p = jnp.pad(t, ((0, 0), (0, 0), (1, 0), (0, 0), (0, 0)))
                return jnp.concatenate([p[:, :, :nw], p[:, :, 1:]], axis=3)
            bk2, bv2 = (look(bk), look(bv))
            seq = jnp.arange(n).reshape(nw, w)
            seq_p = jnp.pad(seq, ((1, 0), (0, 0)), constant_values=-1)
            jt = jnp.concatenate([seq_p[:nw], seq_p[1:]], axis=1)
            it = seq[:, :, None]
            jb = jt[:, None, :]
            mask = (it < jb) | (it > jb + w) | (jb == -1)
            sim = jnp.einsum('bhwie,bhwje->bhwij', bq, bk2) * QK_SCALE
            sim = jnp.where(mask, -jnp.finfo(sim.dtype).max, sim)
            attn = jax.nn.softmax(sim, -1)
            out = jnp.einsum('bhwij,bhwje->bhwie', attn, bv2)
            return out.reshape(b, h, n, d)

        def attn_layer(x, Wqkv, qs, ksc, Wo):
            b, n, _ = x.shape
            qkv = x @ Wqkv
            q, k, v = jnp.split(qkv, 3, -1)
            sh = lambda t: t.reshape(b, n, HEADS, DIM_HEAD).transpose(0, 2, 1, 3)
            q, k, v = (sh(q), sh(k), sh(v))
            q = l2norm(q) * qs
            k = l2norm(k) * ksc
            freqs, scale = rotary_tables(n)
            cos, sin = (jnp.cos(freqs), jnp.sin(freqs))
            q = q * cos * scale + rotate_half(q) * sin * scale
            inv = 1.0 / scale
            k = k * cos * inv + rotate_half(k) * sin * inv
            out = local_attention(q, k, v)
            out = out.transpose(0, 2, 1, 3).reshape(b, n, INNER)
            return out @ Wo

        def ffn_layer(x, g, bln, W1, b1, W2, b2):
            mu = x.mean(-1, keepdims=True)
            var = ((x - mu) ** 2).mean(-1, keepdims=True)
            xn = (x - mu) / jnp.sqrt(var + 1e-05) * g + bln
            hg = xn @ W1 + b1
            a, gate = jnp.split(hg, 2, -1)
            return a * jax.nn.gelu(gate, approximate=False) @ W2 + b2
        key = jax.random.key(seed)
        ks = jax.random.split(key, 8)
        B, N = (2, 256)
        init = lambda k, shape: jax.random.normal(k, shape, jnp.float32) * 0.02
        return {'x': jax.random.normal(ks[0], (B, N, DIM), jnp.float32), 'Wqkv': init(ks[1], (DEPTH, DIM, 3 * INNER)), 'q_scale': jnp.ones((DEPTH, DIM_HEAD), jnp.float32), 'k_scale': jnp.ones((DEPTH, DIM_HEAD), jnp.float32), 'Wo': init(ks[2], (DEPTH, INNER, DIM)), 'ln_g': jnp.ones((DEPTH, DIM), jnp.float32), 'ln_b': jnp.zeros((DEPTH, DIM), jnp.float32), 'W1': init(ks[3], (DEPTH, DIM, 2 * DIM_INNER)), 'b1': jnp.zeros((DEPTH, 2 * DIM_INNER), jnp.float32), 'W2': init(ks[4], (DEPTH, DIM_INNER, DIM)), 'b2': jnp.zeros((DEPTH, DIM), jnp.float32)}
    _L0_ffn_in = _L0_ffn_setup()

    def _L1_attn_setup():
        import jax, jax.numpy as jnp
        import numpy as np
        import math
        D_MODEL = 128
        N_HEAD = 16
        POWER = 2.0
        EPS = 1e-06

        def _alibi_slopes(n_head):
            closest = 2 ** math.floor(math.log2(n_head))
            base = 2 ** (-2 ** (-(math.log2(closest) - 3)))
            slopes = base ** np.arange(1, 1 + closest, dtype=np.float64)
            if closest != n_head:
                extra_base = 2 ** (-2 ** (-(math.log2(2 * closest) - 3)))
                num_rem = min(closest, n_head - closest)
                slopes = np.concatenate([slopes, extra_base ** np.arange(1, 1 + 2 * num_rem, 2, dtype=np.float64)])
            return jnp.asarray(slopes * 4.0, dtype=jnp.float32)
        key = jax.random.key(seed)
        ks = jax.random.split(key, 5)
        B, T, C = (2, 256, D_MODEL)
        x = jax.random.normal(ks[0], (B, T, C), dtype=jnp.float32)
        w_scale = 0.02
        Wq = jax.random.normal(ks[1], (C, C), dtype=jnp.float32) * w_scale
        Wk = jax.random.normal(ks[2], (C, C), dtype=jnp.float32) * w_scale
        Wv = jax.random.normal(ks[3], (C, C), dtype=jnp.float32) * w_scale
        Wo = jax.random.normal(ks[4], (C, C), dtype=jnp.float32) * w_scale
        alibi_slopes = _alibi_slopes(N_HEAD)
        power = jnp.full((1,), POWER, dtype=jnp.float32)
        return {'x': x, 'Wq': Wq, 'Wk': Wk, 'Wv': Wv, 'Wo': Wo, 'alibi_slopes': alibi_slopes, 'power': power}
    _L1_attn_in = _L1_attn_setup()

    def _L1_ffn_setup():
        import jax, jax.numpy as jnp
        import numpy as np
        DIM = 128
        HIDDEN = 384
        SCALE = 1.0 / 127.0

        def _dequant(w_int, dtype):
            return w_int.astype(dtype) * jnp.asarray(SCALE, dtype)
        key = jax.random.key(seed)
        k_x, k_g, k_u, k_d = jax.random.split(key, 4)
        x = jax.random.normal(k_x, (4, 256, DIM), dtype=jnp.float32)
        w_gate = jax.random.randint(k_g, (HIDDEN, DIM), -127, 128, dtype=jnp.int32)
        w_up = jax.random.randint(k_u, (HIDDEN, DIM), -127, 128, dtype=jnp.int32)
        w_down = jax.random.randint(k_d, (DIM, HIDDEN), -127, 128, dtype=jnp.int32)
        return {'x': x, 'w_gate': w_gate, 'w_up': w_up, 'w_down': w_down}
    _L1_ffn_in = _L1_ffn_setup()
    _d = {'L0_attn_x': _L0_attn_in['x'], 'L0_attn_Wq': _L0_attn_in['Wq'], 'L0_attn_Wk': _L0_attn_in['Wk'], 'L0_attn_Wv': _L0_attn_in['Wv'], 'L0_attn_Wp': _L0_attn_in['Wp'], 'L0_attn_bp': _L0_attn_in['bp'], 'L0_attn_conv_w': _L0_attn_in['conv_w'], 'L0_attn_conv_b': _L0_attn_in['conv_b'], 'L0_ffn_Wqkv': _L0_ffn_in['Wqkv'], 'L0_ffn_q_scale': _L0_ffn_in['q_scale'], 'L0_ffn_k_scale': _L0_ffn_in['k_scale'], 'L0_ffn_Wo': _L0_ffn_in['Wo'], 'L0_ffn_ln_g': _L0_ffn_in['ln_g'], 'L0_ffn_ln_b': _L0_ffn_in['ln_b'], 'L0_ffn_W1': _L0_ffn_in['W1'], 'L0_ffn_b1': _L0_ffn_in['b1'], 'L0_ffn_W2': _L0_ffn_in['W2'], 'L0_ffn_b2': _L0_ffn_in['b2'], 'L1_attn_Wq': _L1_attn_in['Wq'], 'L1_attn_Wk': _L1_attn_in['Wk'], 'L1_attn_Wv': _L1_attn_in['Wv'], 'L1_attn_Wo': _L1_attn_in['Wo'], 'L1_attn_alibi_slopes': _L1_attn_in['alibi_slopes'], 'L1_attn_power': _L1_attn_in['power'], 'L1_ffn_w_gate': _L1_ffn_in['w_gate'], 'L1_ffn_w_up': _L1_ffn_in['w_up'], 'L1_ffn_w_down': _L1_ffn_in['w_down']}
    _x0 = _d['L0_attn_x']
    _d['L0_attn_x'] = jax.random.normal(jax.random.fold_in(jax.random.key(seed), 1), (4, 512, 128), dtype=_x0.dtype)
    del _x0
    return _d

def reference(L0_attn_x, L0_attn_Wq, L0_attn_Wk, L0_attn_Wv, L0_attn_Wp, L0_attn_bp, L0_attn_conv_w, L0_attn_conv_b, L0_ffn_Wqkv, L0_ffn_q_scale, L0_ffn_k_scale, L0_ffn_Wo, L0_ffn_ln_g, L0_ffn_ln_b, L0_ffn_W1, L0_ffn_b1, L0_ffn_W2, L0_ffn_b2, L1_attn_Wq, L1_attn_Wk, L1_attn_Wv, L1_attn_Wo, L1_attn_alibi_slopes, L1_attn_power, L1_ffn_w_gate, L1_ffn_w_up, L1_ffn_w_down):

    def _L0_attn_ref(x, Wq, Wk, Wv, Wp, bp, conv_w, conv_b):
        import jax, jax.numpy as jnp
        import numpy as np
        DIM = 128
        HEADS = 16
        HEAD_DIM = DIM // HEADS
        B, S = (4, 512)
        b, s, d = x.shape

        def split_heads(t):
            return t.reshape(b, s, HEADS, HEAD_DIM).transpose(0, 2, 1, 3)
        q = split_heads(x @ Wq.T)
        k = split_heads(x @ Wk.T)
        v = split_heads(x @ Wv.T)
        q = jax.nn.elu(q) + 1.0
        k = jax.nn.elu(k) + 1.0
        kv_state = jnp.einsum('bhnd,bhne->bhde', k, v)
        k_state = k.sum(axis=2)
        attn_out = jnp.einsum('bhnd,bhde->bhne', q, kv_state)
        denom = jnp.maximum(jnp.einsum('bhnd,bhd->bhn', q, k_state), 1e-06)[..., None]
        attn_out = (attn_out / denom).transpose(0, 2, 1, 3).reshape(b, s, d)
        xp = jnp.pad(x, ((0, 0), (1, 1), (0, 0)))
        local = xp[:, :-2, :] * conv_w[:, 0] + xp[:, 1:-1, :] * conv_w[:, 1] + xp[:, 2:, :] * conv_w[:, 2] + conv_b
        return (attn_out + local) @ Wp.T + bp

    def _L0_ffn_ref(x, Wqkv, q_scale, k_scale, Wo, ln_g, ln_b, W1, b1, W2, b2):
        import jax, jax.numpy as jnp
        import numpy as np
        DIM = 128
        DEPTH = 6
        HEADS = 16
        DIM_HEAD = 64
        WINDOW = 32
        INNER = HEADS * DIM_HEAD
        DIM_INNER = int(DIM * 4 * 2 / 3)
        QK_SCALE = 8.0

        def shift_tokens(t):
            a, s = jnp.split(t, 2, -1)
            s = jnp.pad(s, ((0, 0), (1, 0), (0, 0)))[:, :-1]
            return jnp.concatenate([a, s], -1)

        def l2norm(t):
            return t / jnp.maximum(jnp.linalg.norm(t, axis=-1, keepdims=True), 1e-12)

        def rotate_half(x):
            x1, x2 = jnp.split(x, 2, -1)
            return jnp.concatenate([-x2, x1], -1)

        def rotary_tables(n):
            half = jnp.arange(0, DIM_HEAD, 2, dtype=jnp.float32)
            inv_freq = 1.0 / 10000.0 ** (half / DIM_HEAD)
            t = jnp.arange(n, dtype=jnp.float32)
            freqs = t[:, None] * inv_freq[None, :]
            freqs = jnp.concatenate([freqs, freqs], -1)
            base_scale = (half + 0.4 * DIM_HEAD) / (1.4 * DIM_HEAD)
            power = (t - n // 2) / (WINDOW // 2)
            scale = base_scale[None, :] ** power[:, None]
            scale = jnp.concatenate([scale, scale], -1)
            return (freqs, scale)

        def local_attention(q, k, v):
            b, h, n, d = q.shape
            w = WINDOW
            nw = n // w
            bq = q.reshape(b, h, nw, w, d)
            bk = k.reshape(b, h, nw, w, d)
            bv = v.reshape(b, h, nw, w, d)

            def look(t):
                p = jnp.pad(t, ((0, 0), (0, 0), (1, 0), (0, 0), (0, 0)))
                return jnp.concatenate([p[:, :, :nw], p[:, :, 1:]], axis=3)
            bk2, bv2 = (look(bk), look(bv))
            seq = jnp.arange(n).reshape(nw, w)
            seq_p = jnp.pad(seq, ((1, 0), (0, 0)), constant_values=-1)
            jt = jnp.concatenate([seq_p[:nw], seq_p[1:]], axis=1)
            it = seq[:, :, None]
            jb = jt[:, None, :]
            mask = (it < jb) | (it > jb + w) | (jb == -1)
            sim = jnp.einsum('bhwie,bhwje->bhwij', bq, bk2) * QK_SCALE
            sim = jnp.where(mask, -jnp.finfo(sim.dtype).max, sim)
            attn = jax.nn.softmax(sim, -1)
            out = jnp.einsum('bhwij,bhwje->bhwie', attn, bv2)
            return out.reshape(b, h, n, d)

        def attn_layer(x, Wqkv, qs, ksc, Wo):
            b, n, _ = x.shape
            qkv = x @ Wqkv
            q, k, v = jnp.split(qkv, 3, -1)
            sh = lambda t: t.reshape(b, n, HEADS, DIM_HEAD).transpose(0, 2, 1, 3)
            q, k, v = (sh(q), sh(k), sh(v))
            q = l2norm(q) * qs
            k = l2norm(k) * ksc
            freqs, scale = rotary_tables(n)
            cos, sin = (jnp.cos(freqs), jnp.sin(freqs))
            q = q * cos * scale + rotate_half(q) * sin * scale
            inv = 1.0 / scale
            k = k * cos * inv + rotate_half(k) * sin * inv
            out = local_attention(q, k, v)
            out = out.transpose(0, 2, 1, 3).reshape(b, n, INNER)
            return out @ Wo

        def ffn_layer(x, g, bln, W1, b1, W2, b2):
            mu = x.mean(-1, keepdims=True)
            var = ((x - mu) ** 2).mean(-1, keepdims=True)
            xn = (x - mu) / jnp.sqrt(var + 1e-05) * g + bln
            hg = xn @ W1 + b1
            a, gate = jnp.split(hg, 2, -1)
            return a * jax.nn.gelu(gate, approximate=False) @ W2 + b2
        for i in range(DEPTH):
            x = attn_layer(shift_tokens(x), Wqkv[i], q_scale[i], k_scale[i], Wo[i]) + x
            x = ffn_layer(shift_tokens(x), ln_g[i], ln_b[i], W1[i], b1[i], W2[i], b2[i]) + x
        return x

    def _L1_attn_ref(x, Wq, Wk, Wv, Wo, alibi_slopes, power):
        import jax, jax.numpy as jnp
        import numpy as np
        import math
        D_MODEL = 128
        N_HEAD = 16
        POWER = 2.0
        EPS = 1e-06

        def _alibi_slopes(n_head):
            closest = 2 ** math.floor(math.log2(n_head))
            base = 2 ** (-2 ** (-(math.log2(closest) - 3)))
            slopes = base ** np.arange(1, 1 + closest, dtype=np.float64)
            if closest != n_head:
                extra_base = 2 ** (-2 ** (-(math.log2(2 * closest) - 3)))
                num_rem = min(closest, n_head - closest)
                slopes = np.concatenate([slopes, extra_base ** np.arange(1, 1 + 2 * num_rem, 2, dtype=np.float64)])
            return jnp.asarray(slopes * 4.0, dtype=jnp.float32)
        B, T, C = x.shape
        H = N_HEAD
        Dh = C // H
        Q = (x @ Wq.T).reshape(B, T, H, Dh).transpose(0, 2, 1, 3)
        K = (x @ Wk.T).reshape(B, T, H, Dh).transpose(0, 2, 1, 3)
        V = (x @ Wv.T).reshape(B, T, H, Dh).transpose(0, 2, 1, 3)
        scale = 1.0 / Dh ** 0.5 * 16.0
        scores = jnp.einsum('bhqd,bhkd->bhqk', Q, K) * scale
        idx = jnp.arange(T, dtype=jnp.float32)
        distance = idx[None, :] - idx[:, None]
        scores = scores - alibi_slopes[None, :, None, None] * jnp.abs(distance)[None, None]
        scores = jnp.where(distance[None, None] > 0, jnp.float32(-10000.0), scores)
        s = scores / (jnp.abs(scores) + 1.0)
        p = ((s + 1.0) * 0.5) ** power[0]
        probs = p / (p.sum(axis=-1, keepdims=True) + EPS)
        out = jnp.einsum('bhqk,bhkd->bhqd', probs, V)
        out = out.transpose(0, 2, 1, 3).reshape(B, T, C)
        return out @ Wo.T

    def _L1_ffn_ref(x, w_gate, w_up, w_down):
        import jax, jax.numpy as jnp
        import numpy as np
        DIM = 128
        HIDDEN = 384
        SCALE = 1.0 / 127.0

        def _dequant(w_int, dtype):
            return w_int.astype(dtype) * jnp.asarray(SCALE, dtype)
        wg = _dequant(w_gate, x.dtype)
        wu = _dequant(w_up, x.dtype)
        wd = _dequant(w_down, x.dtype)
        gate = jnp.einsum('bsd,hd->bsh', x, wg)
        up = jnp.einsum('bsd,hd->bsh', x, wu)
        h = jax.nn.silu(gate) * up
        return jnp.einsum('bsh,dh->bsd', h, wd)
    x = L0_attn_x
    x = x + _layernorm(_L0_attn_ref(_layernorm(x, axis=-1), L0_attn_Wq, L0_attn_Wk, L0_attn_Wv, L0_attn_Wp, L0_attn_bp, L0_attn_conv_w, L0_attn_conv_b), axis=-1)
    x = x + _layernorm(_L0_ffn_ref(_layernorm(x, axis=-1), L0_ffn_Wqkv, L0_ffn_q_scale, L0_ffn_k_scale, L0_ffn_Wo, L0_ffn_ln_g, L0_ffn_ln_b, L0_ffn_W1, L0_ffn_b1, L0_ffn_W2, L0_ffn_b2), axis=-1)
    x = x + _layernorm(_L1_attn_ref(_layernorm(x, axis=-1), L1_attn_Wq, L1_attn_Wk, L1_attn_Wv, L1_attn_Wo, L1_attn_alibi_slopes, L1_attn_power), axis=-1)
    x = x + _layernorm(_L1_ffn_ref(_layernorm(x, axis=-1), L1_ffn_w_gate, L1_ffn_w_up, L1_ffn_w_down), axis=-1)
    return x

_drawn_inputs = setup_inputs


def setup_inputs(seed=0):
    import zlib

    import numpy as np

    out = dict(_drawn_inputs(seed))
    spreads = {'L0_attn_bp': (0.0, 0.1),
     'L0_attn_conv_b': (0.0, 0.1),
     'L0_ffn_q_scale': (1.0, 0.6),
     'L0_ffn_k_scale': (1.0, 0.6),
     'L0_ffn_ln_g': (1.0, 0.6),
     'L0_ffn_ln_b': (0.0, 0.8),
     'L0_ffn_b1': (0.0, 0.8),
     'L0_ffn_b2': (0.0, 0.1)}
    factors = {'L0_attn_Wq': 5.072, 'L0_ffn_W1': 4.086, 'L0_ffn_W2': 3.992}
    for name, (base, spread) in spreads.items():
        noise = np.random.default_rng([zlib.crc32(name.encode()), seed]).standard_normal(out[name].shape)
        drawn = base * np.exp(spread * noise) if base else spread * noise
        out[name] = jnp.asarray(drawn.astype(out[name].dtype))
    for name, factor in factors.items():
        out[name] = (out[name] * factor).astype(out[name].dtype)
    return out
```

```python
from contextlib import ExitStack

import numpy as np

import concourse.bass as bass
from concourse import mybir

F32 = mybir.dt.float32
BF16 = mybir.dt.bfloat16
I32 = mybir.dt.int32
ALU = mybir.AluOpType
ACT = mybir.ActivationFunctionType
AX = mybir.AxisListType

P = 128
B, N, DIM = 4, 512, 128
TILES = B * N // P
DEPTH, W = 6, 32
INNER2 = int(DIM * 4 * 2 / 3)
STEPS = DEPTH * B
GROUPS = 4 * STEPS
RN_CAP = 1e12 / 2.0 ** 16
LN_EPS = 1e-5
BIG = -1e30
HIDDEN = 384


def add_and_normalise(nc, tag, sems, before, ident, X, yT, XT, x_dram=None, out_dram=None):
    first, last = yT is None, out_dram is not None
    with ExitStack() as ctx:
        sb = lambda name, shape, dt=F32: ctx.enter_context(nc.sbuf_tensor(name + tag, shape, dt))
        ps_y = ctx.enter_context(nc.psum_tensor("ps_y_" + tag, [P, B, 4, DIM], F32))
        ps_x = ctx.enter_context(nc.psum_tensor("ps_x_" + tag, [P, B, N], F32))
        stats = sb("stats", [P, 2, TILES, 6])
        mv = sb("mv", [P, 2, TILES, 2])
        rs = sb("rs", [P, 2, TILES])
        t = sb("t", [P, B, 4, DIM])
        eps = sb("eps", [P, 1])
        rounds = [r for r in (0, 1) if not (first and r == 0) and not (last and r == 1)]
        per = len(rounds)

        def wait(eng, name, value):
            eng.wait_ge(sems[name], before[name] + value)

        with nc.Block() as block:

            @block.sync
            def _(sp):
                if first:
                    for b in range(B):
                        sp.dma_start(X[:, b, :, :], x_dram[b]).then_inc(sems["loaded"], 16)
                        wait(sp, "loaded", 16 * b + 16)
                if last:
                    for b in range(B):
                        wait(sp, "added", b + 1)
                        sp.dma_start(out_dram[b], X[:, b, :, :]).then_inc(sems["stored"], 16)
                    wait(sp, "stored", 16 * B)

            @block.tensor
            def _(pe):
                if not first:
                    for b in range(B):
                        for k in range(4):
                            mm = pe.transpose(ps_y[:, b, k, :], yT[:, b, 1 + P * k:1 + P * k + P], ident[:, :])
                        mm.then_inc(sems["y_turned"], 1)
                if not last:
                    for b in range(B):
                        wait(pe, "scaled", per * b + per)
                        for k in range(4):
                            mm = pe.transpose(ps_x[:, b, P * k:P * k + P], t[:, b, k, :], ident[:, :])
                        mm.then_inc(sems["x_turned"], 1)

            @block.scalar
            def _(act):
                wait(act, "eps_set", 1)
                for b in range(B):
                    for k, r in enumerate(rounds):
                        done = per * b + k + 1
                        wait(act, "aggr", 4 * done)
                        view = rs[:, r, 4 * b:4 * b + 4]
                        act.activation(view, mv[:, r, 4 * b:4 * b + 4, 1], ACT.Ln, bias=eps[:, 0:1]).then_inc(sems["lned"], 1)
                        wait(act, "lned", done)
                        act.activation(view, view, ACT.Exp, scale=-0.5).then_inc(sems["rstd"], 1)
                if not last:
                    for b in range(B):
                        wait(act, "x_turned", b + 1)
                        act.activation(XT[:, b, 1:1 + N], ps_x[:, b, :], ACT.Copy).then_inc(sems["xt_out"], 1)

            @block.vector
            def _(dve):
                dve.memset(eps[:, :], LN_EPS).then_inc(sems["eps_set"], 1)
                if not last:
                    dve.memset(XT[:, :, 0:1], 0.0)
                    dve.memset(XT[:, :, 1 + N:2 + N], 0.0)
                n = 0
                for b in range(B):
                    for r in rounds:
                        n += 1
                        src = X[:, b, :, :] if r else ps_y[:, b, :, :]
                        if r and first:
                            wait(dve, "loaded", 16 * b + 16)
                        elif r:
                            wait(dve, "added", b + 1)
                        else:
                            wait(dve, "y_turned", b + 1)
                        for k in range(4):
                            dve.bn_stats(stats[:, r, 4 * b + k, :], src[:, k, :]).then_inc(sems["stat"], 1)
                        for k in range(4):
                            wait(dve, "stat", 4 * n - 3 + k)
                            dve.bn_aggr(mv[:, r, 4 * b + k, :], stats[:, r, 4 * b + k, :]).then_inc(sems["aggr"], 1)
                        mean = mv[:, r, 4 * b:4 * b + 4, 0:1].broadcast_to([P, 4, DIM])
                        wait(dve, "aggr", 4 * n)
                        if r and not first:
                            wait(dve, "added", b + 1)
                        dve.tensor_tensor(t[:, b, :, :], src, mean, ALU.subtract).then_inc(sems["centred"], 1)
                        wait(dve, "centred", n)
                        wait(dve, "rstd", n)
                        dve.tensor_tensor(t[:, b, :, :], t[:, b, :, :],
                                          rs[:, r, 4 * b:4 * b + 4].unsqueeze(2).broadcast_to([P, 4, DIM]),
                                          ALU.mult).then_inc(sems["scaled"], 1)
                        if not r:
                            wait(dve, "scaled", n)
                            dve.tensor_tensor(X[:, b, :, :], X[:, b, :, :], t[:, b, :, :], ALU.add).then_inc(sems["added"], 1)

        for name, count in (("loaded", 16 * B * first), ("y_turned", B * (not first)), ("stat", 4 * B * per), ("aggr", 4 * B * per),
                            ("lned", B * per), ("rstd", B * per), ("centred", B * per), ("scaled", B * per),
                            ("added", B * (not first)), ("x_turned", B * (not last)), ("stored", 16 * B * last),
                            ("eps_set", 1), ("xt_out", B * (not last))):
            before[name] += count




def over_elements(eng, work):
    work(0)
    with eng.Fori(1, B) as b:
        work(b)


def linear_attention(nc, w, XT, YT):
    with ExitStack() as ctx:
        sb = lambda name, shape, dt=F32: ctx.enter_context(nc.sbuf_tensor("la_" + name, shape, dt))
        ps = lambda name, shape, dt=F32: ctx.enter_context(nc.psum_tensor("la_" + name, shape, dt))
        sem = lambda name: ctx.enter_context(nc.semaphore("la_" + name))
        wq, wkv, wp = sb("wq", [P, DIM]), sb("wkv", [P, 2 * DIM]), sb("wp", [P, DIM])
        vec = sb("vec", [P, 5])
        blocks = sb("blocks", [P, P])
        x = sb("x", [P, N + 2])
        neg = sb("neg", [P, 2, N])
        phi_q, phi_k = sb("phi_q", [P, N]), sb("phi_k", [P, 4, DIM])
        v1 = sb("v1", [P, 4, DIM + 1])
        kv, ks = sb("kv", [P, P]), sb("ks", [P, P])
        den, conv, mix = sb("den", [P, N]), sb("conv", [P, N]), sb("mix", [P, N])
        ps_q, ps_kv = ps("ps_q", [P, N]), ps("ps_kv", [P, 4, 2 * DIM])
        ps_state, ps_num, ps_den, ps_y = ps("ps_state", [P, N]), ps("ps_num", [P, N]), ps("ps_den", [P, N]), ps("ps_y", [P, N])
        loaded, x_in, q_proj, kv_proj, negged, exped, v_out, phi, state, masked = (
            sem(n) for n in ("loaded", "x_in", "q_proj", "kv_proj", "negged", "exped", "v_out", "phi", "state", "masked"))
        nums, capped, lned, recipd, convd, mixed, projected, y_out, ones_set = (
            sem(n) for n in ("nums", "capped", "lned", "recipd", "convd", "mixed", "projected", "y_out", "ones_set"))

        with nc.Block() as block:

            @block.sync
            def _(sp):
                for dst, key in ((wq, "la_wq"), (wkv, "la_wkv"), (wp, "la_wp"), (vec, "la_vec"), (blocks, "la_blocks")):
                    sp.dma_start(dst[:, :], w[key]).then_inc(loaded, 16)

            @block.tensor
            def _(pe):
                pe.wait_ge(loaded, 80)
                pe.wait_ge(ones_set, 1)

                def work(b):
                    pe.wait_ge(x_in, b + 1)
                    pe.matmul(ps_q[:, :], wq[:, :], x[:, 1:1 + N], start=True, stop=True).then_inc(q_proj, 1)
                    for t in range(4):
                        mm = pe.matmul(ps_kv[:, t, :], x[:, 1 + P * t:1 + P * t + P], wkv[:, :],
                                       start=(t % 2 == 0), stop=True, skip_group_check=True)
                    mm.then_inc(kv_proj, 1)
                    pe.wait_ge(phi, b * 2 + 2)
                    pe.wait_ge(v_out, b + 1)
                    for t in range(4):
                        mm = pe.matmul(ps_state[:, 0:DIM + 1], phi_k[:, t, :], v1[:, t, :], start=(t == 0), stop=(t == 3))
                    mm.then_inc(state, 1)
                    pe.wait_ge(masked, b * 2 + 2)
                    pe.matmul(ps_den[:, :], ks[:, :], phi_q[:, :], start=True, stop=True).then_inc(nums, 1)
                    pe.matmul(ps_num[:, :], kv[:, :], phi_q[:, :], start=True, stop=True).then_inc(nums, 1)
                    pe.wait_ge(mixed, b * 2 + 2)
                    pe.matmul(ps_y[:, :], wp[:, :], mix[:, :], start=True, stop=True).then_inc(projected, 1)

                over_elements(pe, work)

            @block.scalar
            def _(act):
                act.wait_ge(loaded, 80)

                def work(b):
                    act.wait_ge(kv_proj, b + 1)
                    act.activation(v1[:, :, 0:DIM], ps_kv[:, :, DIM:], ACT.Copy).then_inc(v_out, 1)
                    act.wait_ge(negged, b * 2 + 2)
                    act.activation(neg[:, :, :], neg[:, :, :], ACT.Exp).then_inc(exped, 1)
                    act.wait_ge(capped, b + 1)
                    act.activation(den[:, :], den[:, :], ACT.Ln).then_inc(lned, 1)
                    act.wait_ge(lned, b + 1)
                    act.activation(den[:, :], den[:, :], ACT.Exp, scale=-1.0).then_inc(recipd, 1)
                    act.wait_ge(projected, b + 1)
                    act.activation(YT[:, b, 1:1 + N], ps_y[:, :], ACT.Identity, bias=vec[:, 4:5]).then_inc(y_out, 1)

                act.preload_act_table_set("natural_log_exp_and_others")
                over_elements(act, work)

            @block.vector
            def _(dve):
                dve.memset(v1[:, :, DIM:], 1.0).then_inc(ones_set, 1)
                dve.wait_ge(loaded, 80)

                def work(b):
                    if not isinstance(b, int):
                        dve.wait_ge(y_out, b)
                    dve.tensor_copy(x[:, :], XT[:, b, :]).then_inc(x_in, 1)
                    dve.wait_ge(q_proj, b + 1)
                    dve.tensor_scalar(neg[:, 0, :], ps_q[:, :], 0.0, None, ALU.min).then_inc(negged, 1)
                    dve.wait_ge(kv_proj, b + 1)
                    dve.wait_ge(v_out, b + 1)
                    dve.tensor_scalar(neg[:, 1, :].rearrange("p (t c) -> p t c", t=4), ps_kv[:, :, 0:DIM],
                                      0.0, None, ALU.min).then_inc(negged, 1)
                    dve.wait_ge(x_in, b + 1)
                    dve.tensor_scalar(conv[:, :], x[:, 0:N], vec[:, 0:1], vec[:, 3:4], ALU.mult, ALU.add).then_inc(convd, 1)
                    for k in (1, 2):
                        dve.wait_ge(convd, b * 3 + k)
                        dve.scalar_tensor_tensor(out=conv[:, :], in0=x[:, k:k + N], scalar=vec[:, k:k + 1], in1=conv[:, :],
                                                 op0=ALU.mult, op1=ALU.add).then_inc(convd, 1)
                    dve.wait_ge(exped, b + 1)
                    dve.scalar_tensor_tensor(out=phi_k[:, :, :], in0=ps_kv[:, :, 0:DIM], scalar=0.0,
                                             in1=neg[:, 1, :].rearrange("p (t c) -> p t c", t=4),
                                             op0=ALU.max, op1=ALU.add).then_inc(phi, 1)
                    dve.scalar_tensor_tensor(out=phi_q[:, :], in0=ps_q[:, :], scalar=0.0, in1=neg[:, 0, :],
                                             op0=ALU.max, op1=ALU.add).then_inc(phi, 1)
                    dve.wait_ge(state, b + 1)
                    dve.tensor_scalar(ks[:, :], blocks[:, :], ps_state[:, DIM:DIM + 1], None, ALU.mult).then_inc(masked, 1)
                    dve.tensor_tensor(kv[:, :], blocks[:, :], ps_state[:, 0:DIM], ALU.mult).then_inc(masked, 1)
                    dve.wait_ge(nums, b * 2 + 1)
                    dve.tensor_scalar(den[:, :], ps_den[:, :], 1e-6, None, ALU.max).then_inc(capped, 1)
                    dve.wait_ge(recipd, b + 1)
                    dve.wait_ge(nums, b * 2 + 2)
                    dve.tensor_tensor(mix[:, :], den[:, :], ps_num[:, :], ALU.mult).then_inc(mixed, 1)
                    dve.wait_ge(mixed, b * 2 + 1)
                    dve.wait_ge(convd, b * 3 + 3)
                    dve.tensor_tensor(mix[:, :], mix[:, :], conv[:, :], ALU.add).then_inc(mixed, 1)

                over_elements(dve, work)


def windowed_attention_stack(nc, w, XT):
    with ExitStack() as ctx:
        sb = lambda name, shape, dt=F32: ctx.enter_context(nc.sbuf_tensor(name, shape, dt))
        ps = lambda name, shape, dt=F32: ctx.enter_context(nc.psum_tensor(name, shape, dt))
        sem = lambda name: ctx.enter_context(nc.semaphore(name))

        w_qkv = sb("w_qkv", [P, 4, 768])
        w_o = sb("w_o", [P, 8, DIM])
        w_up = sb("w_up", [P, 2 * INNER2])
        w_down = sb("w_down", [P, 3, DIM])
        qk_gain = sb("qk_gain", [P, 4])
        ffn_vec = sb("ffn_vec", [P, 9])
        cos_t = sb("cos_t", [P, 2, N])
        sin_t = sb("sin_t", [P, 2, N])
        head_ones = sb("head_ones", [P, P])
        mean_ones = sb("mean_ones", [P, P])
        ident16 = sb("ident16", [P, P], BF16)
        mask16 = sb("mask16", [P, N], BF16)
        xs = sb("xs", [P, N])
        tab_c = sb("tab_c", [P, 2, 2, N])
        tab_s = sb("tab_s", [P, 2, 2, N])
        sq = sb("sq", [P, 2, 2, N])
        sqs = sb("sqs", [P, 2, N])
        rn = sb("rn", [P, 2, N])
        qkn = sb("qkn", [P, 2, 2, N])
        qkc = sb("qkc", [P, 2, 2, N])
        qkr = sb("qkr", [P, 2, 2, N])
        pair = sb("pair", [P, 2, 2, 2, W + N])
        prob = sb("prob", [P, 16, 2, W])
        probT = sb("probT", [P, 16, 2, W])
        band = sb("band", [P, 2, 16, 5 * W])
        smax = sb("smax", [P, 16])
        ssum = sb("ssum", [P, 16])
        srec = sb("srec", [P, 16])
        v_sb = sb("v_sb", [P, 4, 4, 256])
        o_sb = sb("o_sb", [P, 8, N])
        x1 = sb("x1", [P, 1 + N])
        xs2 = sb("xs2", [P, N])
        cen = sb("cen", [P, N])
        cen2 = sb("cen2", [P, N])
        rstd = sb("rstd", [P, N])
        xn = sb("xn", [P, N])
        hid = sb("hid", [P, 3, N])
        eps_b = sb("eps_b", [P, 2])

        ps_qk = ps("ps_qk", [P, 2, 2, N])
        ps_s = ps("ps_s", [P, 2, N])
        ps_w = ps("ps_w", [P, 2, N])

        head_w = [sem(f"head_w{s}") for s in range(4)]
        gain_w = sem("gain_w")
        wo_w, up_w, down_w, vec_w = sem("wo_w"), sem("up_w"), sem("down_w"), sem("vec_w")
        const_w = sem("const_w")
        zeroed = sem("zeroed")
        xs_ready = sem("xs_ready")
        qk_proj = sem("qk_proj")
        squared = sem("squared")
        sq_added = sem("sq_added")
        norm_summed = sem("norm_summed")
        norm_ln = sem("norm_ln")
        rnorm = sem("rnorm")
        tables = sem("tables")
        normed = sem("normed")
        turned = sem("turned")
        rotated = sem("rotated")
        paired = [sem("paired0"), sem("paired1")]
        scored = sem("scored")
        maxed = sem("maxed")
        shifted = sem("shifted")
        exped = sem("exped")
        summed = sem("summed")
        recipd = sem("recipd")
        scaled = sem("scaled")
        flipped = sem("flipped")
        banded = sem("banded")
        v_proj = sem("v_proj")
        v_out = sem("v_out")
        pv_done = sem("pv_done")
        o_out = sem("o_out")
        wo_done = sem("wo_done")
        x1_done = sem("x1_done")
        xs2_done = sem("xs2_done")
        mean_done = sem("mean_done")
        cen_done = sem("cen_done")
        cen2_done = sem("cen2_done")
        var_done = sem("var_done")
        var_ln = sem("var_ln")
        rstd_done = sem("rstd_done")
        xn_half = sem("xn_half")
        xn_done = sem("xn_done")
        up_done = sem("up_done")
        gelu_done = sem("gelu_done")
        hid_done = sem("hid_done")
        down_done = sem("down_done")
        x_done = sem("x_done")

        def live(i, s, lag):
            return not isinstance(i, int) or 0 <= 4 * i + s - lag < GROUPS

        def tail_live(i):
            return not isinstance(i, int) or 0 <= i - 2 < STEPS

        def upto(i, s, lag, per=1, part=None):
            part = per if part is None else part
            if isinstance(i, int):
                n = 4 * i + s - lag
                if n < 0:
                    return None
                if n >= GROUPS:
                    return per * GROUPS
                return per * n + part
            return i * (4 * per) + (per * (s - lag) + part)

        def step(i, lag, per=1, part=None):
            part = per if part is None else part
            if isinstance(i, int):
                k = i - lag
                if k < 0:
                    return None
                return per * min(k, STEPS - 1) + part if k < STEPS else per * STEPS
            return i * per + (part - per * lag)

        def wait(eng, s, value):
            if value is not None:
                eng.wait_ge(s, value)

        def layer_of(i, lag=0):
            return (i - lag) // 4 + 1 if isinstance(i, int) else ((i - lag) >> 2) + 1

        def run(eng, slots):
            for i in (0, 1):
                slots(i)
            with eng.Fori(2, STEPS) as i:
                slots(i)
            for i in (STEPS, STEPS + 1):
                slots(i)

        with nc.Block() as block:

            @block.sync
            def _(sp):
                def after(s, value):
                    if value is not None:
                        sp.wait_ge(s, value)
                        sp.wait_ge(zeroed, 4)

                def load_group(layer, s):
                    sp.dma_start(w_qkv[:, s, :], w["w_qkv"][layer, s]).then_inc(head_w[s], 16)

                def load_rest(layer, used=None):
                    after(wo_done, used)
                    sp.dma_start(w_o[:, :, :], w["w_o"][layer]).then_inc(wo_w, 16)
                    after(up_done, None if used is None else used * 6)
                    sp.dma_start(w_up[:, :], w["w_up"][layer]).then_inc(up_w, 16)
                    after(x_done, None if used is None else used + B)
                    sp.dma_start(w_down[:, :, :], w["w_down"][layer]).then_inc(down_w, 16)
                    sp.dma_start(ffn_vec[:, :], w["ffn_vec"][layer]).then_inc(vec_w, 16)

                def load_gain(layer):
                    sp.dma_start(qk_gain[:, :], w["qk_gain"][layer]).then_inc(gain_w, 16)

                def pair_up(n, s):
                    par = s % 2
                    after(rotated, n + 1)
                    for h in range(4):
                        for half in range(2):
                            to = 64 * (h % 2) + 32 * half
                            sp.dma_start(pair[to:to + 32, par, :, h // 2, W:],
                                         qkr[32 * h:32 * h + 32, :, half, :]).then_inc(paired[par], 16)

                sp.wait_ge(zeroed, 4)
                load_group(0, 0)
                sp.dma_start(head_ones[:, :], w["head_ones"]).then_inc(const_w, 16)
                sp.dma_start(mean_ones[:, :], w["mean_ones"]).then_inc(const_w, 16)
                sp.dma_start(ident16[:, :], w["ident16"]).then_inc(const_w, 16)
                sp.dma_start(mask16[:, :], w["mask16"]).then_inc(const_w, 16)
                sp.dma_start(cos_t[:, :, :], w["cos_t"]).then_inc(const_w, 16)
                sp.dma_start(sin_t[:, :, :], w["sin_t"]).then_inc(const_w, 16)
                load_gain(0)
                for s in range(1, 4):
                    load_group(0, s)
                load_rest(0)

                def layer_steps(layer):
                    for b in range(4):
                        i = layer * 4 + b
                        for s in range(4):
                            if not isinstance(layer, int) or i + s > 0:
                                pair_up(i * 4 + (s - 1), s - 1)
                            if b == 3 and (not isinstance(layer, int) or layer < DEPTH - 1):
                                after(v_proj, i * 8 + (2 * s + 2))
                                load_group(layer + 1, s)
                                if s == 3:
                                    after(tables, i + 1)
                                    load_gain(layer + 1)
                        if b == 1 and (not isinstance(layer, int) or layer > 0):
                            load_rest(layer, layer * 4)

                layer_steps(0)
                with sp.Fori(1, DEPTH - 1) as layer:
                    layer_steps(layer)
                layer_steps(DEPTH - 1)
                pair_up(GROUPS - 1, 3)
                sp.wait_ge(x_done, B + STEPS)

            @block.tensor
            def _(pe):
                pe.wait_ge(const_w, 96)

                def project_qk(i, s):
                    if s == 0:
                        wait(pe, xs_ready, step(i, 0))
                    pe.wait_ge(head_w[s], layer_of(i) * 16)
                    wait(pe, normed, upto(i, s, 1, 2))
                    for x in range(2):
                        for half in range(2):
                            c = (2 * x + half) * P
                            mm = pe.matmul(ps_qk[:, x, half, :], w_qkv[:, s, c:c + P], xs[:, :],
                                           start=True, stop=True)
                        mm.then_inc(qk_proj, 1)

                def project_v(i, s):
                    for k in range(2):
                        wait(pe, o_out, upto(i, s, 4, 2, k + 1))
                        wait(pe, norm_ln, upto(i, s, 1))
                        for t in (2 * k, 2 * k + 1):
                            mm = pe.matmul(ps_w[:, k, (t % 2) * 256:(t % 2) * 256 + 256],
                                           xs[:, t * P:t * P + P], w_qkv[:, s, 512:768],
                                           start=(t % 2 == 0), stop=True, skip_group_check=True)
                        mm.then_inc(v_proj, 1)

                def sum_norms(i, s):
                    wait(pe, sq_added, upto(i, s, 0))
                    for x in range(2):
                        wait(pe, v_out, upto(i, s, 0, 2, x + 1))
                        pe.matmul(ps_w[:, x, :], head_ones[:, :], sqs[:, x, :],
                                  start=True, stop=True).then_inc(norm_summed, 1)

                def score(i, s):
                    par = s % 2
                    wait(pe, shifted, upto(i, s, 3))
                    if isinstance(i, int):
                        pe.wait_ge(paired[par], 128 * ((4 * i + s - 2) // 2 + 1))
                    else:
                        pe.wait_ge(paired[par], i * 256 + 128 * ((s - 2) // 2 + 1))
                    for e in range(2):
                        pe.matmul(ps_s[:, e, :], ident16[:, :], mask16[:, :], start=True, stop=False,
                                  skip_group_check=True)
                    for t in range(4):
                        for p in range(2):
                            for wd in range(4):
                                for e in range(2):
                                    r = slice(64 * e, 64 * e + 64)
                                    tok = P * t + W * wd
                                    c = (2 * t + p) * 2 * W
                                    mm = pe.matmul(ps_s[W * wd:W * wd + W, e, c:c + 2 * W],
                                                   pair[r, par, 0, p, W + tok:2 * W + tok],
                                                   pair[r, par, 1, p, tok:tok + 2 * W],
                                                   start=False, stop=True, skip_group_check=True)
                    mm.then_inc(scored, 1)

                def values(i, s):
                    par = s % 2
                    wait(pe, banded, upto(i, s, 4))
                    wait(pe, norm_ln, upto(i, s, 1))
                    wait(pe, o_out, upto(i, s, 5, 2))
                    if s == 0:
                        wait(pe, x1_done, step(i, 2))
                    elif s == 1:
                        wait(pe, cen_done, step(i, 2))
                    elif s == 2:
                        wait(pe, var_ln, step(i, 2))
                    else:
                        wait(pe, hid_done, step(i, 2, 3))
                    for p in range(2):
                        for t in range(4):
                            width = min(5 * W, N - P * t)
                            for e in range(2):
                                mm = pe.matmul(ps_w[64 * e:64 * e + 64, p, P * t:P * t + width],
                                               v_sb[:, s, t, (2 * p + e) * 64:(2 * p + e) * 64 + 64],
                                               band[:, par, e * 8 + 2 * t + p, 0:width],
                                               start=(t == 0), stop=(t == 3), skip_group_check=True)
                        mm.then_inc(pv_done, 1)

                def attn_out(i):
                    wait(pe, o_out, upto(i, 0, 5, 2))
                    pe.wait_ge(wo_w, layer_of(i, 2) * 16)
                    wait(pe, norm_ln, upto(i, 0, 1))
                    before = step(i, 3)
                    wait(pe, x_done, None if before is None else before + B)
                    for c in range(8):
                        mm = pe.matmul(ps_w[:, 0, :], w_o[:, c, :], o_sb[:, c, :], start=(c == 0), stop=(c == 7))
                    mm.then_inc(wo_done, 1)

                def mean(i):
                    wait(pe, xs2_done, step(i, 2))
                    wait(pe, norm_ln, upto(i, 1, 1))
                    wait(pe, o_out, upto(i, 1, 5, 2))
                    pe.matmul(ps_w[:, 0, :], mean_ones[:, :], xs2[:, :], start=True, stop=True).then_inc(mean_done, 1)

                def variance(i):
                    wait(pe, cen2_done, step(i, 2))
                    wait(pe, norm_ln, upto(i, 1, 0))
                    wait(pe, o_out, upto(i, 1, 4, 2))
                    pe.matmul(ps_w[:, 0, :], mean_ones[:, :], cen2[:, :], start=True, stop=True).then_inc(var_done, 1)

                def up(i):
                    wait(pe, xn_done, step(i, 2))
                    pe.wait_ge(up_w, layer_of(i, 2) * 16)
                    wait(pe, norm_ln, upto(i, 2, 0))
                    wait(pe, o_out, upto(i, 2, 4, 2))
                    for k, (gate, c) in enumerate(((1, 0), (1, 1), (0, 0), (0, 1), (1, 2), (0, 2))):
                        m = min(P, INNER2 - P * c)
                        if k in (2, 3):
                            wait(pe, gelu_done, step(i, 2, 3, k - 1))
                        elif k in (4, 5):
                            wait(pe, hid_done, step(i, 2, 3, k - 3))
                        f = gate * INNER2 + P * c
                        pe.matmul(ps_w[0:m, k % 2, :], w_up[:, f:f + m], xn[:, :],
                                  start=True, stop=True).then_inc(up_done, 1)

                def down(i):
                    wait(pe, hid_done, step(i, 2, 3))
                    pe.wait_ge(down_w, layer_of(i, 2) * 16)
                    wait(pe, norm_ln, upto(i, 3, 0))
                    wait(pe, o_out, upto(i, 3, 4, 2))
                    for c in range(3):
                        m = min(P, INNER2 - P * c)
                        mm = pe.matmul(ps_w[:, 0, :], w_down[0:m, c, :], hid[0:m, c, :], start=(c == 0), stop=(c == 2))
                    mm.then_inc(down_done, 1)

                def slots(i):
                    for s in range(4):
                        tail = tail_live(i)
                        if tail and s == 0:
                            attn_out(i)
                        if tail and s == 1:
                            mean(i)
                        if live(i, s, 0):
                            project_qk(i, s)
                        if live(i, s, 4):
                            values(i, s)
                        if live(i, s, 0):
                            project_v(i, s)
                            sum_norms(i, s)
                        if tail and s == 1:
                            variance(i)
                        if tail and s == 2:
                            up(i)
                        if tail and s == 3:
                            down(i)
                        if live(i, s, 2):
                            score(i, s)

                run(pe, slots)

            @block.scalar
            def _(act):
                act.wait_ge(zeroed, 4)

                def shift_in(i, step_index):
                    b = i % 4 if isinstance(i, int) else i & 3
                    act.wait_ge(x_done, i + 1)
                    if not isinstance(i, int) or i > 0:
                        act.wait_ge(v_proj, i * 8)
                    act.activation(xs[0:64, :], XT[0:64, b, 1:1 + N], ACT.Copy)
                    act.activation(xs[64:128, :], XT[64:128, b, 0:N], ACT.Copy).then_inc(xs_ready, 1)

                def squares(i, s):
                    wait(act, sq_added, upto(i, s, 1))
                    for x in range(2):
                        wait(act, qk_proj, upto(i, s, 0, 2, x + 1))
                        act.activation(sq[:, x, :, :], ps_qk[:, x, :, :], ACT.Square).then_inc(squared, 1)

                def values_out(i, s):
                    if s == 0:
                        wait(act, wo_done, step(i, 2))
                    for p in range(2):
                        wait(act, pv_done, upto(i, s, 4, 2, p + 1))
                        act.activation(o_sb[:, 2 * s + p, :], ps_w[:, p, :], ACT.Copy).then_inc(o_out, 1)

                def v_copy(i, s):
                    for k in range(2):
                        wait(act, v_proj, upto(i, s, 0, 2, k + 1))
                        act.activation(v_sb[:, s, 2 * k:2 * k + 2, :], ps_w[:, k, :], ACT.Copy).then_inc(v_out, 1)

                def rnorms(i, s):
                    wait(act, norm_summed, upto(i, s, 0, 2))
                    wait(act, normed, upto(i, s, 1, 2))
                    act.activation(rn[:, :, :], ps_w[:, :, :], ACT.Ln, bias=eps_b[:, 0:1], scale=2.0 ** 32).then_inc(norm_ln, 1)
                    wait(act, norm_ln, upto(i, s, 0))
                    act.activation(rn[:, :, :], rn[:, :, :], ACT.Exp, scale=-0.5).then_inc(rnorm, 1)

                def exps(i, s):
                    wait(act, shifted, upto(i, s, 2))
                    act.activation(prob[:, :, :, :], prob[:, :, :, :], ACT.Exp).then_inc(exped, 1)

                def bands(i, s):
                    par = (s - 3) % 2
                    wait(act, flipped, upto(i, s, 3))
                    wait(act, pv_done, upto(i, s, 5, 2))
                    for wd in range(4):
                        rows = slice(W * wd, W * wd + W)
                        act.activation(band[rows, par, :, W * wd:W * wd + W], probT[rows, :, 1, :], ACT.Copy)
                        if wd:
                            before = slice(W * wd - W, W * wd)
                            act.activation(band[before, par, :, W * wd:W * wd + W], probT[rows, :, 0, :], ACT.Copy)
                    for e in range(2):
                        last = act.activation(band[96:128, par, 8 * e:8 * e + 6, 4 * W:5 * W],
                                              probT[0:32, 8 * e + 2:8 * e + 8, 0, :], ACT.Copy)
                    last.then_inc(banded, 1)

                def shift_mid(i):
                    wait(act, x1_done, step(i, 2))
                    act.activation(xs2[0:64, :], x1[0:64, 1:1 + N], ACT.Copy)
                    act.activation(xs2[64:128, :], x1[64:128, 0:N], ACT.Copy).then_inc(xs2_done, 1)

                def centred_square(i):
                    wait(act, cen_done, step(i, 2))
                    act.activation(cen2[:, :], cen[:, :], ACT.Square).then_inc(cen2_done, 1)

                def rstds(i):
                    wait(act, var_done, step(i, 2))
                    act.activation(rstd[:, :], ps_w[:, 0, :], ACT.Ln, bias=eps_b[:, 1:2]).then_inc(var_ln, 1)
                    wait(act, var_ln, step(i, 2))
                    act.activation(rstd[:, :], rstd[:, :], ACT.Exp, scale=-0.5).then_inc(rstd_done, 1)

                def gelus(i):
                    pe_chunk = (0, 1, 4)
                    for c in range(3):
                        m = min(P, INNER2 - P * c)
                        wait(act, up_done, step(i, 2, 6, pe_chunk[c] + 1))
                        act.activation(hid[0:m, c, :], ps_w[0:m, pe_chunk[c] % 2, :], ACT.Gelu,
                                       bias=ffn_vec[0:m, 5 + c:6 + c]).then_inc(gelu_done, 1)

                def slots(i):
                    tail = tail_live(i)
                    for s in range(4):
                        if s == 0 and live(i, 0, 0):
                            shift_in(i, i)
                        if live(i, s, 0):
                            squares(i, s)
                        if tail and s == 0:
                            shift_mid(i)
                        if live(i, s, 4):
                            values_out(i, s)
                        if tail and s == 1:
                            centred_square(i)
                        if live(i, s, 0):
                            v_copy(i, s)
                            rnorms(i, s)
                        if tail and s == 1:
                            rstds(i)
                        if live(i, s, 3):
                            bands(i, s)
                        if tail and s == 2:
                            wait(act, vec_w, layer_of(i, 2) * 16)
                            gelus(i)
                            act.preload_act_table_set("natural_log_exp_and_others")
                        if live(i, s, 2):
                            exps(i, s)

                act.preload_act_table_set("natural_log_exp_and_others")
                run(act, slots)

            @block.vector
            def _(dve):
                dve.memset(pair[:, :, :, :, 0:W], 0.0).then_inc(zeroed, 1)
                dve.memset(x1[:, 0:1], 0.0).then_inc(zeroed, 1)
                dve.memset(eps_b[:, 1:2], LN_EPS).then_inc(x_done, B)
                dve.memset(eps_b[:, 0:1], 2.0 ** -62).then_inc(zeroed, 1)
                dve.memset(band[:, :, :, :], 0.0).then_inc(zeroed, 1)
                dve.wait_ge(zeroed, 4)

                def normalise(i, s):
                    wait(dve, rotated, upto(i, s, 2))
                    wait(dve, rnorm, upto(i, s, 1))
                    for x in range(2):
                        r = rn[:, x:x + 1, :].broadcast_to([P, 2, N])
                        dve.scalar_tensor_tensor(out=qkn[:, x, :, :], in0=r, scalar=RN_CAP, in1=ps_qk[:, x, :, :],
                                                 op0=ALU.min, op1=ALU.mult).then_inc(normed, 1)

                def turn(i, s):
                    wait(dve, normed, upto(i, s, 1, 2))
                    if (s - 1) % 4 == 0:
                        wait(dve, tables, step(i, 0))
                    flat = lambda a: a[:, :, :, :].rearrange("p x h n -> p (x h n)")
                    dve.tensor_tensor(flat(qkc), flat(qkn), flat(tab_c), ALU.mult).then_inc(turned, 1)
                    dve.tensor_tensor(flat(qkn), flat(qkn), flat(tab_s), ALU.mult).then_inc(turned, 1)

                def maxima(i, s):
                    wait(dve, scored, upto(i, s, 2))
                    view = ps_s[:, :, :].rearrange("p e (c k) -> p (e c) k", k=2 * W)
                    dve.tensor_reduce(smax[:, :], view, AX.X, ALU.max).then_inc(maxed, 1)
                    wait(dve, maxed, upto(i, s, 2))
                    wait(dve, flipped, upto(i, s, 3))
                    dve.tensor_tensor(prob[:, :, :, :].rearrange("p c w k -> p c (w k)"), view,
                                      smax[:, :].unsqueeze(2).broadcast_to([P, 16, 2 * W]),
                                      ALU.subtract).then_inc(shifted, 1)

                def sums(i, s):
                    wait(dve, exped, upto(i, s, 3))
                    dve.tensor_reduce(ssum[:, :], prob[:, :, :, :].rearrange("p c w k -> p c (w k)"), AX.X, ALU.add).then_inc(summed, 1)
                    wait(dve, summed, upto(i, s, 3))
                    wait(dve, scaled, upto(i, s, 4))
                    dve.reciprocal(srec[:, :], ssum[:, :]).then_inc(recipd, 1)

                def flip(i, s):
                    wait(dve, scaled, upto(i, s, 3))
                    wait(dve, banded, upto(i, s, 4))
                    dve.transpose(probT[:, :, :, :].rearrange("p c w k -> p (c w k)"),
                                  prob[:, :, :, :].rearrange("p c w k -> p (c w k)")).then_inc(flipped, 1)

                def slots(i):
                    tail = tail_live(i)
                    for s in range(4):
                        bj = (i - 2) % 4 if isinstance(i, int) else (i - 2) & 3
                        if live(i, s, 1):
                            normalise(i, s)
                        if tail and s == 0:
                            wait(dve, wo_done, step(i, 2))
                            dve.tensor_tensor(x1[:, 1:1 + N], XT[:, bj, 1:1 + N], ps_w[:, 0, :], ALU.add).then_inc(x1_done, 1)
                        if tail and s == 1:
                            wait(dve, mean_done, step(i, 2))
                            dve.tensor_tensor(cen[:, :], xs2[:, :], ps_w[:, 0, :], ALU.subtract).then_inc(cen_done, 1)
                        if live(i, s, 3):
                            sums(i, s)
                        if live(i, s, 1):
                            turn(i, s)
                        if live(i, s, 3):
                            flip(i, s)
                        if tail and s == 1:
                            wait(dve, rstd_done, step(i, 2))
                            dve.wait_ge(vec_w, layer_of(i, 2) * 16)
                            dve.scalar_tensor_tensor(out=xn[:, :], in0=cen[:, :], scalar=ffn_vec[:, 0:1], in1=rstd[:, :],
                                                     op0=ALU.mult, op1=ALU.mult).then_inc(xn_half, 1)
                            wait(dve, xn_half, step(i, 2))
                            dve.tensor_scalar(xn[:, :], xn[:, :], ffn_vec[:, 1:2], None, ALU.add).then_inc(xn_done, 1)
                        if tail and s == 2:
                            chunk = (2, 3, 5)
                            for c in range(3):
                                m = min(P, INNER2 - P * c)
                                wait(dve, up_done, step(i, 2, 6, chunk[c] + 1))
                                wait(dve, gelu_done, step(i, 2, 3, c + 1))
                                dve.scalar_tensor_tensor(out=hid[0:m, c, :], in0=ps_w[0:m, chunk[c] % 2, :],
                                                         scalar=ffn_vec[0:m, 2 + c:3 + c], in1=hid[0:m, c, :],
                                                         op0=ALU.add, op1=ALU.mult).then_inc(hid_done, 1)
                        if tail and s == 3:
                            wait(dve, down_done, step(i, 2))
                            dve.scalar_tensor_tensor(out=XT[:, bj, 1:1 + N], in0=ps_w[:, 0, :], scalar=ffn_vec[:, 8:9],
                                                     in1=x1[:, 1:1 + N], op0=ALU.add, op1=ALU.add).then_inc(x_done, 1)
                        if live(i, s, 2):
                            maxima(i, s)

                run(dve, slots)

            @block.gpsimd
            def _(pool):
                pool.wait_ge(const_w, 96)

                def make_tables(i):
                    for x in range(2):
                        for half in range(2):
                            g = qk_gain[:, 2 * x + half:2 * x + half + 1]
                            pool.tensor_scalar(tab_c[:, x, half, :], cos_t[:, x, :], g, 1.0, ALU.mult, ALU.mult)
                            last = pool.tensor_scalar(tab_s[:, x, half, :], sin_t[:, x, :], g,
                                                      -1.0 if half else 1.0, ALU.mult, ALU.mult)
                    last.then_inc(tables, 1)

                def add_squares(i, s):
                    wait(pool, norm_summed, upto(i, s, 1, 2))
                    wait(pool, squared, upto(i, s, 0, 2))
                    pool.tensor_tensor(sqs[:, :, :], sq[:, :, 0, :], sq[:, :, 1, :], ALU.add).then_inc(sq_added, 1)

                def add_turned(i, s):
                    wait(pool, turned, upto(i, s, 1, 2))
                    wait(pool, scored, upto(i, s, 3))
                    if isinstance(i, int):
                        if 4 * i + s >= 2:
                            pool.wait_ge(paired[s % 2], 128 * ((4 * i + s - 2) // 2 + 1))
                    else:
                        pool.wait_ge(paired[s % 2], i * 256 + 128 * ((s - 2) // 2 + 1))
                    pool.tensor_tensor(qkr[:, :, 0, :], qkc[:, :, 0, :], qkn[:, :, 1, :], ALU.add)
                    pool.tensor_tensor(qkr[:, :, 1, :], qkc[:, :, 1, :], qkn[:, :, 0, :], ALU.add).then_inc(rotated, 1)

                def scale_probs(i, s):
                    wait(pool, recipd, upto(i, s, 3))
                    view = prob[:, :, :, :].rearrange("p c w k -> p c (w k)")
                    pool.tensor_tensor(view, view, srec[:, :].unsqueeze(2).broadcast_to([P, 16, 2 * W]),
                                       ALU.mult).then_inc(scaled, 1)

                def slots(i):
                    for s in range(4):
                        if live(i, s, 3):
                            scale_probs(i, s)
                        if live(i, s, 0):
                            add_squares(i, s)
                        if s == 0 and live(i, 0, 0):
                            pool.wait_ge(gain_w, layer_of(i) * 16)
                        if live(i, s, 1):
                            add_turned(i, s)
                        if s == 0 and live(i, 0, 0):
                            make_tables(i)

                run(pool, slots)


def power_attention(nc, w, XT, YT):
    with ExitStack() as ctx:
        sb = lambda name, shape, dt=F32: ctx.enter_context(nc.sbuf_tensor("pa_" + name, shape, dt))
        ps = lambda name, shape, dt=F32: ctx.enter_context(nc.psum_tensor("pa_" + name, shape, dt))
        sem = lambda name: ctx.enter_context(nc.semaphore("pa_" + name))
        wq, wk = sb("wq", [P, 16, 32]), sb("wk", [P, 16, 32])
        wv = sb("wv", [P, DIM])
        wo = sb("wo", [P, 4, DIM])
        dist = sb("dist", [P, N])
        slopes, power = sb("slopes", [P, 16]), sb("power", [P, 1])
        cst = sb("cst", [P, 4])
        ones = sb("ones", [P, 32])
        tick = sb("tick", [P, 16])
        eps6 = sb("eps6", [P, 1])
        x = sb("x", [P, N])
        v_pad = sb("v_pad", [P, 4, 16, 32])
        qT, kT = sb("qT", [P, 2, N]), sb("kT", [P, 2, N])
        z = sb("z", [P, 3, 4, N])
        a = sb("a", [P, 3, 4, N])
        pk = sb("pk", [P, 4, 4, N])
        rd = sb("rd", [P, N])
        oT = sb("oT", [P, 4, N])
        ps_s = ps("ps_s", [P, 4, N])
        ps_p = ps("ps_p", [P, 2, N])
        ps_o, ps_d = ps("ps_o", [P, N]), ps("ps_d", [P, N])
        names = ("loaded", "zeroed", "filled", "x_in", "v_proj", "v_out", "proj", "q_out", "k_out", "scored", "zd", "masked",
                 "absd", "relud", "lned", "subd", "exped", "valued", "den_ln", "den_r", "o_out", "projected", "y_out", "set_up")
        (loaded, zeroed, filled, x_in, v_proj, v_out, proj, q_out, k_out, scored, zd, masked,
         absd, relud, lned, subd, exped, valued, den_ln, den_r, o_out, projected, y_out, set_up) = map(sem, names)
        UNITS = 16

        def unit_wait(eng, s, b, u, per=1, part=None):
            part = per if part is None else part
            if isinstance(b, int) and UNITS * b + u < 0:
                return
            eng.wait_ge(s, b * (UNITS * per) + (per * u + part))

        with nc.Block() as block:

            @block.sync
            def _(sp):
                sp.wait_ge(zeroed, 3)
                with nc.allow_non_contiguous_dma(reason="32-byte runs of head columns, once"):
                    sp.dma_start(wq[:, :, 0:8], w["pa_wq"].rearrange("c (h d) -> c h d", d=8)).then_inc(loaded, 16)
                    sp.dma_start(wk[:, :, 0:8], w["pa_wk"].rearrange("c (h d) -> c h d", d=8)).then_inc(loaded, 16)
                    for c in range(4):
                        sp.dma_start(wo[32 * c:32 * c + 8, :, :],
                                     w["pa_wo"].rearrange("(g c d) o -> c d g o", c=4, d=8)[c]).then_inc(loaded, 16)
                sp.dma_start(wv[:, :], w["pa_wv"]).then_inc(loaded, 16)
                sp.dma_start(dist[:, :], w["pa_dist"]).then_inc(loaded, 16)
                sp.dma_start(slopes[:, :], w["pa_slopes"]).then_inc(loaded, 16)
                sp.dma_start(power[:, :], w["pa_power"]).then_inc(loaded, 16)

            @block.tensor
            def _(pe):
                pe.wait_ge(loaded, 160)
                pe.wait_ge(set_up, 3)

                def project(b, g):
                    for k, (wt, out) in enumerate(((wq, q_out), (wk, k_out))):
                        if g or not isinstance(b, int):
                            pe.wait_ge(out, b * 4 + g)
                        if g == 0 and not isinstance(b, int):
                            pe.wait_ge(y_out, b)
                        if g == 0:
                            pe.wait_ge(v_out, b * 4 + 4)
                        pe.matmul(ps_p[:, k, :], wt[:, 4 * g:4 * g + 4, :].rearrange("c h d -> c (h d)"), x[:, :],
                                  start=True, stop=True).then_inc(proj, 1)

                def score(b, g, kt):
                    u = 4 * g + kt
                    n = N - P * kt
                    if kt == 0:
                        pe.wait_ge(q_out, b * 4 + (g + 1))
                        pe.wait_ge(k_out, b * 4 + (g + 1))
                    unit_wait(pe, zd, b, u - 1, 4)
                    for c in range(4):
                        r = slice(32 * c, 32 * c + 32)
                        mm = pe.matmul(ps_s[:, c, 0:n], kT[r, g % 2, P * kt:P * kt + P], qT[r, g % 2, P * kt:N],
                                       start=True, stop=True)
                        mm.then_inc(scored, 1)

                def values(b, u):
                    g, kt = u // 4, u % 4
                    unit_wait(pe, exped, b, u)
                    if kt == 0 and (g or not isinstance(b, int)):
                        pe.wait_ge(o_out, b * 4 + g)
                    for c in range(4):
                        pe.matmul(ps_o[32 * c:32 * c + 32, :], v_pad[:, kt, 4 * g + c, :], pk[:, kt, c, :],
                                  start=(kt == 0), stop=(kt == 3), skip_group_check=True)
                        mm = pe.matmul(ps_d[32 * c:32 * c + 32, :], ones[:, :], pk[:, kt, c, :],
                                       start=(kt == 0), stop=(kt == 3), skip_group_check=True)
                    mm.then_inc(valued, 1)

                def work(b):
                    pe.wait_ge(x_in, b + 1)
                    if not isinstance(b, int):
                        pe.wait_ge(y_out, b)
                    for t in range(4):
                        pe.matmul(ps_p[:, 0, P * t:P * t + P], x[:, P * t:P * t + P], wv[:, :],
                                  start=(t == 0), stop=True, skip_group_check=True).then_inc(v_proj, 1)
                    project(b, 0)
                    for u in range(UNITS):
                        score(b, u // 4, u % 4)
                        if u % 4 == 2 and u < 12:
                            project(b, u // 4 + 1)
                        if u >= 2:
                            values(b, u - 2)
                    values(b, UNITS - 2)
                    values(b, UNITS - 1)
                    pe.wait_ge(o_out, b * 4 + 4)
                    for g in range(4):
                        mm = pe.matmul(ps_p[:, 0, :], wo[:, g, :], oT[:, g, :], start=(g == 0), stop=(g == 3))
                    mm.then_inc(projected, 1)

                over_elements(pe, work)

            @block.scalar
            def _(act):
                act.wait_ge(set_up, 1)
                act.wait_ge(loaded, 160)
                act.activation(cst[:, 1:2], cst[:, 1:2], ACT.Ln, bias=1.0).then_inc(filled, 1)
                act.wait_ge(filled, 1)
                act.wait_ge(set_up, 2)
                act.activation(cst[:, 2:3], cst[:, 1:2], ACT.Exp, bias=cst[:, 0:1], scale=cst[:, 3:4]).then_inc(filled, 1)

                def project_out(b, g):
                    act.wait_ge(proj, b * 8 + (2 * g + 1))
                    if g >= 2:
                        act.wait_ge(scored, b * 64 + (16 * g - 16))
                    act.activation(qT[:, g % 2, :], ps_p[:, 0, :], ACT.Copy, scale=16.0 / 8.0 ** 0.5).then_inc(q_out, 1)
                    act.wait_ge(proj, b * 8 + (2 * g + 2))
                    act.activation(kT[:, g % 2, :], ps_p[:, 1, :], ACT.Copy).then_inc(k_out, 1)

                def logs(b, u):
                    n, par = N - P * (u % 4), u % 3
                    unit_wait(act, absd, b, u)
                    act.activation(a[:, par, :, 0:n], a[:, par, :, 0:n], ACT.Ln, bias=1.0)
                    act.activation(z[:, par, :, 0:n], z[:, par, :, 0:n], ACT.Ln, bias=1.0).then_inc(lned, 1)

                def weights(b, u):
                    kt, par = u % 4, u % 3
                    unit_wait(act, subd, b, u)
                    unit_wait(act, valued, b, u - 4)
                    act.activation(pk[:, kt, :, P * kt:N], z[:, par, :, 0:N - P * kt], ACT.Exp,
                                   bias=cst[:, 0:1], scale=power[:, 0:1]).then_inc(exped, 1)

                def recip_sum(b, g):
                    unit_wait(act, valued, b, 4 * g + 3)
                    if g or not isinstance(b, int):
                        act.wait_ge(o_out, b * 4 + g)
                    act.activation(rd[:, :], ps_d[:, :], ACT.Ln, bias=eps6[:, 0:1]).then_inc(den_ln, 1)
                    act.wait_ge(den_ln, b * 4 + (g + 1))
                    act.activation(rd[:, :], rd[:, :], ACT.Exp, scale=-1.0).then_inc(den_r, 1)

                def work(b):
                    for t in range(4):
                        act.wait_ge(v_proj, b * 4 + (t + 1))
                        if t == 3:
                            act.activation(v_pad[:, :, :, 0:8],
                                           ps_p[:, 0, :].rearrange("p (t h d) -> p t h d", t=4, d=8), ACT.Copy).then_inc(v_out, 4)
                    project_out(b, 0)
                    for u in range(UNITS + 4):
                        if u < UNITS:
                            logs(b, u)
                        if u % 4 == 2 and u < 12:
                            project_out(b, u // 4 + 1)
                        if 1 <= u <= UNITS:
                            weights(b, u - 1)
                        if u >= 5 and (u - 5) % 4 == 0:
                            recip_sum(b, (u - 5) // 4)
                    act.wait_ge(projected, b + 1)
                    act.activation(YT[:, b, 1:1 + N], ps_p[:, 0, :], ACT.Copy).then_inc(y_out, 1)

                over_elements(act, work)

            @block.vector
            def _(dve):
                dve.memset(wq[:, :, :], 0.0).then_inc(zeroed, 1)
                dve.memset(wk[:, :, :], 0.0).then_inc(zeroed, 1)
                dve.memset(wo[:, :, :], 0.0).then_inc(zeroed, 1)
                dve.memset(v_pad[:, :, :, :], 0.0)
                dve.memset(eps6[:, :], 1e-6)
                dve.memset(ones[:, :], 1.0)
                dve.memset(cst[:, 1:2], 10000.0).then_inc(set_up, 1)
                dve.wait_ge(loaded, 160)
                dve.tensor_scalar(cst[:, 0:1], power[:, :], -float(np.log(2.0)), None, ALU.mult)
                dve.tensor_scalar(cst[:, 3:4], power[:, :], -1.0, None, ALU.mult).then_inc(set_up, 1)
                dve.memset(pk[:, 1:4, :, 0:3 * P], 1.0).then_inc(zeroed, 1)
                dve.wait_ge(zeroed, 4)
                dve.wait_ge(filled, 2)
                for kt in range(1, 4):
                    last = dve.tensor_scalar(pk[:, kt, :, 0:P * kt], pk[:, kt, :, 0:P * kt], cst[:, 2:3], None, ALU.mult)
                last.then_inc(set_up, 1)

                def negated(b, u):
                    g, n, par = u // 4, N - P * (u % 4), u % 3
                    unit_wait(dve, exped, b, u - 3 if u else -1)
                    for c in range(4):
                        unit_wait(dve, scored, b, u, 4, c + 1)
                        dve.scalar_tensor_tensor(out=z[:, par, c, 0:n], in0=dist[:, 0:n], scalar=slopes[:, 4 * g + c:4 * g + c + 1],
                                                 in1=ps_s[:, c, 0:n], op0=ALU.mult, op1=ALU.subtract).then_inc(zd, 1)

                def parts(b, u):
                    n, par = N - P * (u % 4), u % 3
                    unit_wait(dve, masked, b, u)
                    dve.tensor_scalar(a[:, par, :, 0:n], z[:, par, :, 0:n], -2.0, 0.0, ALU.mult, ALU.max).then_inc(relud, 1)
                    unit_wait(dve, relud, b, u)
                    dve.tensor_tensor(z[:, par, :, 0:n], z[:, par, :, 0:n], a[:, par, :, 0:n], ALU.add).then_inc(absd, 1)

                def heads_out(b, g):
                    dve.wait_ge(den_r, b * 4 + (g + 1))
                    if g == 0 and not isinstance(b, int):
                        dve.wait_ge(projected, b)
                    dve.tensor_tensor(oT[:, g, :], rd[:, :], ps_o[:, :], ALU.mult).then_inc(o_out, 1)

                def work(b):
                    if not isinstance(b, int):
                        dve.wait_ge(proj, b * 8)
                    dve.tensor_copy(x[:, :], XT[:, b, 1:1 + N]).then_inc(x_in, 1)
                    for u in range(UNITS + 4):
                        if u < UNITS:
                            negated(b, u)
                        if 1 <= u <= UNITS:
                            parts(b, u - 1)
                        if u >= 6 and (u - 6) % 4 == 0:
                            heads_out(b, (u - 6) // 4)

                over_elements(dve, work)

            @block.gpsimd
            def _(pool):
                pool.wait_ge(set_up, 3)

                def mask(b, u):
                    unit_wait(pool, zd, b, u, 4)
                    pool.tensor_tensor(tick[:, u:u + 1], ones[:, 0:1], ones[:, 0:1], ALU.mult)
                    view = z[:, u % 3, :, 0:P]
                    pool.affine_select(out=view, in_=view, compare_op=ALU.is_ge, fill=10000.0, base=0,
                                       pattern=[[0, 4], [1, P]], channel_multiplier=-1).then_inc(masked, 1)

                def subtract(b, u):
                    n, par = N - P * (u % 4), u % 3
                    unit_wait(pool, lned, b, u)
                    pool.tensor_tensor(z[:, par, :, 0:n], a[:, par, :, 0:n], z[:, par, :, 0:n], ALU.subtract).then_inc(subd, 1)

                def work(b):
                    for u in range(UNITS + 1):
                        if u < UNITS:
                            mask(b, u)
                        if u >= 1:
                            subtract(b, u - 1)

                over_elements(pool, work)


def swiglu(nc, w, XT, YT):
    chunks = HIDDEN // P
    with ExitStack() as ctx:
        sb = lambda name, shape, dt=F32: ctx.enter_context(nc.sbuf_tensor("sg_" + name, shape, dt))
        ps = lambda name, shape, dt=F32: ctx.enter_context(nc.psum_tensor("sg_" + name, shape, dt))
        sem = lambda name: ctx.enter_context(nc.semaphore("sg_" + name))
        raw = sb("raw", [P, 3, HIDDEN], I32)
        wf = sb("wf", [P, 3, HIDDEN])
        act_g = sb("act_g", [P, chunks, N])
        h = sb("h", [P, chunks, N])
        ps_g, ps_u, ps_y = ps("ps_g", [P, chunks, N]), ps("ps_u", [P, chunks, N]), ps("ps_y", [P, N])
        loaded, dequant, gated, upped, silued, hid, downed, y_out = (
            sem(n) for n in ("loaded", "dequant", "gated", "upped", "silued", "hid", "downed", "y_out"))

        with nc.Block() as block:

            @block.sync
            def _(sp):
                for k, key in enumerate(("sg_gate", "sg_up", "sg_down")):
                    sp.dma_start(raw[:, k, :], w[key]).then_inc(loaded, 16)

            @block.tensor
            def _(pe):
                pe.wait_ge(dequant, 1)

                def work(b):
                    for c in range(chunks):
                        for k, (bank, done, used, n_used) in enumerate(((ps_g, gated, silued, 1), (ps_u, upped, hid, 1))):
                            if not isinstance(b, int):
                                pe.wait_ge(used, b * chunks + (c + 1 - chunks))
                            pe.matmul(bank[:, c, :], wf[:, k, P * c:P * c + P], XT[:, b, 1:1 + N],
                                      start=True, stop=True).then_inc(done, 1)
                    if not isinstance(b, int):
                        pe.wait_ge(y_out, b)
                    for c in range(chunks):
                        pe.wait_ge(hid, b * chunks + (c + 1))
                        mm = pe.matmul(ps_y[:, :], wf[:, 2, P * c:P * c + P], h[:, c, :], start=(c == 0), stop=(c == chunks - 1))
                    mm.then_inc(downed, 1)

                over_elements(pe, work)

            @block.scalar
            def _(act):
                def work(b):
                    for c in range(chunks):
                        act.wait_ge(gated, b * chunks + (c + 1))
                        act.activation(act_g[:, c, :], ps_g[:, c, :], ACT.Silu).then_inc(silued, 1)
                    act.wait_ge(downed, b + 1)
                    act.activation(YT[:, b, 1:1 + N], ps_y[:, :], ACT.Copy).then_inc(y_out, 1)

                over_elements(act, work)

            @block.vector
            def _(dve):
                dve.wait_ge(loaded, 48)
                dve.tensor_scalar(wf[:, :, :], raw[:, :, :], float(np.float32(1.0 / 127.0)), None, ALU.mult).then_inc(dequant, 1)

                def work(b):
                    for c in range(chunks):
                        dve.wait_ge(silued, b * chunks + (c + 1))
                        dve.wait_ge(upped, b * chunks + (c + 1))
                        if c == 0 and not isinstance(b, int):
                            dve.wait_ge(downed, b)
                        dve.tensor_tensor(h[:, c, :], act_g[:, c, :], ps_u[:, c, :], ALU.mult).then_inc(hid, 1)

                over_elements(dve, work)


def build(nc, a, out):
    with ExitStack() as ctx:
        sb = lambda name, shape, dt=F32: ctx.enter_context(nc.sbuf_tensor(name, shape, dt))
        X = sb("X", [P, B, 4, DIM])
        XT = sb("XT", [P, B, N + 2])
        ident = sb("ident", [P, P])
        iload = ctx.enter_context(nc.semaphore("iload"))
        with nc.Block() as block:
            @block.sync
            def _(sp):
                sp.dma_start(ident[:, :], a["ident"]).then_inc(iload, 16)
                sp.wait_ge(iload, 16)
        sems = {name: ctx.enter_context(nc.semaphore("ln_" + name)) for name in (
            "loaded", "y_turned", "stat", "aggr", "lned", "rstd", "centred", "scaled", "added", "x_turned", "stored",
            "eps_set", "xt_out")}
        before = dict.fromkeys(sems, 0)
        tok = lambda d: d.rearrange("b (k p) c -> b p k c", p=P)
        add_and_normalise(nc, "_0", sems, before, ident, X, None, XT, x_dram=tok(a["x"]))
        with nc.sbuf_tensor("YT_a", [P, B, N + 2], F32) as YT:
            linear_attention(nc, a, XT, YT)
            add_and_normalise(nc, "_1", sems, before, ident, X, YT, XT)
        windowed_attention_stack(nc, a, XT)
        with nc.sbuf_tensor("YT_b", [P, B, N + 2], F32) as YT:
            add_and_normalise(nc, "_2", sems, before, ident, X, XT, YT)
            power_attention(nc, a, YT, XT)
            add_and_normalise(nc, "_3", sems, before, ident, X, XT, YT)
            swiglu(nc, a, YT, XT)
            add_and_normalise(nc, "_4", sems, before, ident, X, XT, None, out_dram=tok(out))


def rotary():
    f = np.float32
    half = np.arange(0, 64, 2, dtype=f)
    t = np.arange(N, dtype=f)
    freqs = t[:, None] * (f(1.0) / f(10000.0) ** (half / f(64)))[None, :]
    base = (half + f(0.4 * 64)) / f(1.4 * 64)
    scale = base[None, :] ** ((t - N // 2) / f(W // 2))[:, None]
    def lay(table):
        q, k = table * scale * f(8 * 65536), table * (f(1.0) / scale) * f(65536)
        return np.ascontiguousarray(np.tile(np.stack([q.T, k.T], 1), (4, 1, 1)).astype(f))
    return lay(np.cos(freqs)), lay(np.sin(freqs))


def constants():
    i = np.arange(P)
    f = np.float32
    q, key = np.meshgrid(i % W, np.arange(2 * W), indexing="ij")
    ok = (q <= key) & (key <= q + W)
    first = ok & ~((i[:, None] < W) & (key < W))
    m = np.stack([first, first, *[ok] * 6], 1)
    cos, sin = rotary()
    return {
        "ident": np.eye(P, dtype=f),
        "ident16": np.eye(P).astype(mybir.dt.np(BF16)),
        "head_ones": (i[:, None] // W == i[None, :] // W).astype(f),
        "mean_ones": np.full((P, P), 1.0 / DIM, f),
        "mask16": np.where(m, 0.0, BIG).reshape(P, N).astype(mybir.dt.np(BF16)),
        "la_blocks": (i[:, None] // 8 == i[None, :] // 8).astype(f),
        "pa_dist": (np.arange(N)[None, :] - i[:, None]).astype(f),
        "cos_t": cos, "sin_t": sin,
    }


def lay_out(inp):
    f = lambda k: np.asarray(inp[k])
    Wqkv = f("L0_ffn_Wqkv")
    halves = lambda m: m.reshape(DEPTH, DIM, 4, 4, 2, 32).transpose(0, 2, 1, 4, 3, 5).reshape(DEPTH, 4, DIM, 256)
    v = Wqkv[:, :, 2048:].reshape(DEPTH, DIM, 4, 256).transpose(0, 2, 1, 3)
    gains = lambda m: np.tile(m.reshape(DEPTH, 2, 32).transpose(0, 2, 1), (1, 4, 1))
    pad = lambda m, n: np.concatenate([m, np.zeros((m.shape[0], n - m.shape[1], *m.shape[2:]), m.dtype)], 1)
    b1 = f("L0_ffn_b1").reshape(DEPTH, 2, INNER2).transpose(0, 2, 1)
    b1 = pad(b1, 3 * P).reshape(DEPTH, 3, P, 2).transpose(0, 2, 3, 1).reshape(DEPTH, P, 6)
    col = lambda k: f(k)[..., None]
    return {
        "x": f("L0_attn_x"),
        "la_wq": f("L0_attn_Wq").T,
        "la_wkv": np.concatenate([f("L0_attn_Wk").T, f("L0_attn_Wv").T], 1),
        "la_wp": f("L0_attn_Wp").T,
        "la_vec": np.concatenate([f("L0_attn_conv_w"), col("L0_attn_conv_b"), col("L0_attn_bp")], 1),
        "w_qkv": np.concatenate([halves(Wqkv[:, :, :1024]), halves(Wqkv[:, :, 1024:2048]), v], 3),
        "w_o": f("L0_ffn_Wo").reshape(DEPTH, 8, P, DIM).transpose(0, 2, 1, 3),
        "w_up": f("L0_ffn_W1"),
        "w_down": pad(f("L0_ffn_W2"), 3 * P).reshape(DEPTH, 3, P, DIM).transpose(0, 2, 1, 3),
        "qk_gain": np.concatenate([gains(f("L0_ffn_q_scale")), gains(f("L0_ffn_k_scale"))], 2),
        "ffn_vec": np.concatenate([col("L0_ffn_ln_g"), col("L0_ffn_ln_b"), b1, col("L0_ffn_b2")], 2),
        "pa_wq": f("L1_attn_Wq").T, "pa_wk": f("L1_attn_Wk").T, "pa_wv": f("L1_attn_Wv").T, "pa_wo": f("L1_attn_Wo").T,
        "pa_slopes": np.tile(f("L1_attn_alibi_slopes")[None], (P, 1)),
        "pa_power": np.tile(f("L1_attn_power")[None], (P, 1)),
        "sg_gate": f("L1_ffn_w_gate").T, "sg_up": f("L1_ffn_w_up").T,
        "sg_down": f("L1_ffn_w_down").T.reshape(HIDDEN // P, P, DIM).transpose(1, 0, 2).reshape(P, HIDDEN),
    }


def kernel(**inputs):
    import concourse.bacc as bacc
    from concourse.bass_utils import run_bass_kernel_spmd as launch
    nc = bacc.Bacc("TRN2", target_bir_lowering=False, num_devices=1)
    arrays = {**lay_out(inputs), **constants()}
    arrays = {k: np.ascontiguousarray(v) for k, v in arrays.items()}
    aps = {k: nc.dram_tensor("in_" + k, v.shape, mybir.dt.from_np(v.dtype), kind="ExternalInput").ap()
           for k, v in arrays.items()}
    out = nc.dram_tensor("out_0", (B, N, DIM), F32, kind="ExternalOutput").ap()
    build(nc, aps, out)
    r = launch(nc, [{"in_" + k: v for k, v in arrays.items()}], core_ids=[0])
    return r.results[0]["out_0"]
```

```python
from contextlib import ExitStack

import numpy as np

import concourse.bass as bass
from concourse import mybir

F32 = mybir.dt.float32
BF16 = mybir.dt.bfloat16
I32 = mybir.dt.int32
ALU = mybir.AluOpType
ACT = mybir.ActivationFunctionType
AX = mybir.AxisListType

P = 128
B, N, DIM = 4, 512, 128
TILES = B * N // P
DEPTH, W = 6, 32
INNER2 = int(DIM * 4 * 2 / 3)
STEPS = DEPTH * B
GROUPS = 4 * STEPS
RN_CAP = 1e12 / 2.0 ** 16
LN_EPS = 1e-5
BIG = -1e30
HIDDEN = 384


def add_and_normalise(nc, tag, sems, before, ident, X, yT, XT, x_dram=None, out_dram=None):
    first, last = yT is None, out_dram is not None
    with ExitStack() as ctx:
        sb = lambda name, shape, dt=F32: ctx.enter_context(nc.sbuf_tensor(name + tag, shape, dt))
        ps_y = ctx.enter_context(nc.psum_tensor("ps_y_" + tag, [P, B, 4, DIM], F32))
        ps_x = ctx.enter_context(nc.psum_tensor("ps_x_" + tag, [P, B, N], F32))
        stats = sb("stats", [P, 2, TILES, 6])
        mv = sb("mv", [P, 2, TILES, 2])
        rs = sb("rs", [P, 2, TILES])
        t = sb("t", [P, B, 4, DIM])
        eps = sb("eps", [P, 1])
        rounds = [r for r in (0, 1) if not (first and r == 0) and not (last and r == 1)]
        per = len(rounds)

        def wait(eng, name, value):
            eng.wait_ge(sems[name], before[name] + value)

        with nc.Block() as block:

            @block.sync
            def _(sp):
                if first:
                    for b in range(B):
                        sp.dma_start(X[:, b, :, :], x_dram[b]).then_inc(sems["loaded"], 16)
                        wait(sp, "loaded", 16 * b + 16)
                if last:
                    for b in range(B):
                        wait(sp, "added", b + 1)
                        sp.dma_start(out_dram[b], X[:, b, :, :]).then_inc(sems["stored"], 16)
                    wait(sp, "stored", 16 * B)

            @block.tensor
            def _(pe):
                if not first:
                    for b in range(B):
                        for k in range(4):
                            mm = pe.transpose(ps_y[:, b, k, :], yT[:, b, 1 + P * k:1 + P * k + P], ident[:, :])
                        mm.then_inc(sems["y_turned"], 1)
                if not last:
                    for b in range(B):
                        wait(pe, "scaled", per * b + per)
                        for k in range(4):
                            mm = pe.transpose(ps_x[:, b, P * k:P * k + P], t[:, b, k, :], ident[:, :])
                        mm.then_inc(sems["x_turned"], 1)

            @block.scalar
            def _(act):
                wait(act, "eps_set", 1)
                for b in range(B):
                    for k, r in enumerate(rounds):
                        done = per * b + k + 1
                        wait(act, "aggr", 4 * done)
                        view = rs[:, r, 4 * b:4 * b + 4]
                        act.activation(view, mv[:, r, 4 * b:4 * b + 4, 1], ACT.Ln, bias=eps[:, 0:1]).then_inc(sems["lned"], 1)
                        wait(act, "lned", done)
                        act.activation(view, view, ACT.Exp, scale=-0.5).then_inc(sems["rstd"], 1)
                if not last:
                    for b in range(B):
                        wait(act, "x_turned", b + 1)
                        act.activation(XT[:, b, 1:1 + N], ps_x[:, b, :], ACT.Copy).then_inc(sems["xt_out"], 1)

            @block.vector
            def _(dve):
                dve.memset(eps[:, :], LN_EPS).then_inc(sems["eps_set"], 1)
                if not last:
                    dve.memset(XT[:, :, 0:1], 0.0)
                    dve.memset(XT[:, :, 1 + N:2 + N], 0.0)
                n = 0
                for b in range(B):
                    for r in rounds:
                        n += 1
                        src = X[:, b, :, :] if r else ps_y[:, b, :, :]
                        if r and first:
                            wait(dve, "loaded", 16 * b + 16)
                        elif r:
                            wait(dve, "added", b + 1)
                        else:
                            wait(dve, "y_turned", b + 1)
                        for k in range(4):
                            dve.bn_stats(stats[:, r, 4 * b + k, :], src[:, k, :]).then_inc(sems["stat"], 1)
                        for k in range(4):
                            wait(dve, "stat", 4 * n - 3 + k)
                            dve.bn_aggr(mv[:, r, 4 * b + k, :], stats[:, r, 4 * b + k, :]).then_inc(sems["aggr"], 1)
                        mean = mv[:, r, 4 * b:4 * b + 4, 0:1].broadcast_to([P, 4, DIM])
                        wait(dve, "aggr", 4 * n)
                        if r and not first:
                            wait(dve, "added", b + 1)
                        dve.tensor_tensor(t[:, b, :, :], src, mean, ALU.subtract).then_inc(sems["centred"], 1)
                        wait(dve, "centred", n)
                        wait(dve, "rstd", n)
                        dve.tensor_tensor(t[:, b, :, :], t[:, b, :, :],
                                          rs[:, r, 4 * b:4 * b + 4].unsqueeze(2).broadcast_to([P, 4, DIM]),
                                          ALU.mult).then_inc(sems["scaled"], 1)
                        if not r:
                            wait(dve, "scaled", n)
                            dve.tensor_tensor(X[:, b, :, :], X[:, b, :, :], t[:, b, :, :], ALU.add).then_inc(sems["added"], 1)

        for name, count in (("loaded", 16 * B * first), ("y_turned", B * (not first)), ("stat", 4 * B * per), ("aggr", 4 * B * per),
                            ("lned", B * per), ("rstd", B * per), ("centred", B * per), ("scaled", B * per),
                            ("added", B * (not first)), ("x_turned", B * (not last)), ("stored", 16 * B * last),
                            ("eps_set", 1), ("xt_out", B * (not last))):
            before[name] += count




def over_elements(eng, work):
    work(0)
    with eng.Fori(1, B) as b:
        work(b)


def linear_attention(nc, w, XT, YT):
    with ExitStack() as ctx:
        sb = lambda name, shape, dt=F32: ctx.enter_context(nc.sbuf_tensor("la_" + name, shape, dt))
        ps = lambda name, shape, dt=F32: ctx.enter_context(nc.psum_tensor("la_" + name, shape, dt))
        sem = lambda name: ctx.enter_context(nc.semaphore("la_" + name))
        wq, wkv, wp = sb("wq", [P, DIM]), sb("wkv", [P, 2 * DIM]), sb("wp", [P, DIM])
        vec = sb("vec", [P, 5])
        blocks = sb("blocks", [P, P])
        x = sb("x", [P, N + 2])
        neg = sb("neg", [P, 2, N])
        phi_q, phi_k = sb("phi_q", [P, N]), sb("phi_k", [P, 4, DIM])
        v1 = sb("v1", [P, 4, DIM + 1])
        kv, ks = sb("kv", [P, P]), sb("ks", [P, P])
        den, conv, mix = sb("den", [P, N]), sb("conv", [P, N]), sb("mix", [P, N])
        ps_q, ps_kv = ps("ps_q", [P, N]), ps("ps_kv", [P, 4, 2 * DIM])
        ps_state, ps_num, ps_den, ps_y = ps("ps_state", [P, N]), ps("ps_num", [P, N]), ps("ps_den", [P, N]), ps("ps_y", [P, N])
        loaded, x_in, q_proj, kv_proj, negged, exped, v_out, phi, state, masked = (
            sem(n) for n in ("loaded", "x_in", "q_proj", "kv_proj", "negged", "exped", "v_out", "phi", "state", "masked"))
        nums, capped, lned, recipd, convd, mixed, projected, y_out, ones_set = (
            sem(n) for n in ("nums", "capped", "lned", "recipd", "convd", "mixed", "projected", "y_out", "ones_set"))

        def in_steps(eng, front, step):
            front(0)
            step(0)
            with eng.Fori(1, B - 1) as b:
                step(b)
            step(B - 1, more=False)

        with nc.Block() as block:

            @block.sync
            def _(sp):
                for dst, key in ((wq, "la_wq"), (wkv, "la_wkv"), (wp, "la_wp"), (vec, "la_vec"), (blocks, "la_blocks")):
                    sp.dma_start(dst[:, :], w[key]).then_inc(loaded, 16)

            @block.tensor
            def _(pe):
                pe.wait_ge(loaded, 80)
                pe.wait_ge(ones_set, 1)

                def front(b):
                    pe.wait_ge(x_in, b + 1)
                    pe.matmul(ps_q[:, :], wq[:, :], x[:, 1:1 + N], start=True, stop=True).then_inc(q_proj, 1)
                    for t in range(4):
                        mm = pe.matmul(ps_kv[:, t, :], x[:, 1 + P * t:1 + P * t + P], wkv[:, :],
                                       start=(t % 2 == 0), stop=True, skip_group_check=True)
                    mm.then_inc(kv_proj, 1)

                def step(b, more=True):
                    pe.wait_ge(phi, b * 2 + 2)
                    pe.wait_ge(v_out, b + 1)
                    for t in range(4):
                        mm = pe.matmul(ps_state[:, 0:DIM + 1], phi_k[:, t, :], v1[:, t, :], start=(t == 0), stop=(t == 3))
                    mm.then_inc(state, 1)
                    if more:
                        front(b + 1)
                    pe.wait_ge(masked, b * 2 + 2)
                    pe.matmul(ps_den[:, :], ks[:, :], phi_q[:, :], start=True, stop=True).then_inc(nums, 1)
                    pe.matmul(ps_num[:, :], kv[:, :], phi_q[:, :], start=True, stop=True).then_inc(nums, 1)
                    pe.wait_ge(mixed, b * 2 + 2)
                    if not isinstance(b, int) or b > 0:
                        pe.wait_ge(y_out, b)
                    pe.matmul(ps_y[:, :], wp[:, :], mix[:, :], start=True, stop=True).then_inc(projected, 1)

                in_steps(pe, front, step)

            @block.scalar
            def _(act):
                act.wait_ge(loaded, 80)

                def front(b):
                    act.wait_ge(kv_proj, b + 1)
                    act.activation(v1[:, :, 0:DIM], ps_kv[:, :, DIM:], ACT.Copy).then_inc(v_out, 1)
                    act.wait_ge(negged, b * 2 + 2)
                    act.activation(neg[:, :, :], neg[:, :, :], ACT.Exp).then_inc(exped, 1)

                def step(b, more=True):
                    if more:
                        front(b + 1)
                    act.wait_ge(capped, b + 1)
                    act.activation(den[:, :], den[:, :], ACT.Ln).then_inc(lned, 1)
                    act.wait_ge(lned, b + 1)
                    act.activation(den[:, :], den[:, :], ACT.Exp, scale=-1.0).then_inc(recipd, 1)
                    act.wait_ge(projected, b + 1)
                    act.activation(YT[:, b, 1:1 + N], ps_y[:, :], ACT.Identity, bias=vec[:, 4:5]).then_inc(y_out, 1)

                act.preload_act_table_set("natural_log_exp_and_others")
                in_steps(act, front, step)

            @block.vector
            def _(dve):
                dve.memset(v1[:, :, DIM:], 1.0).then_inc(ones_set, 1)
                dve.wait_ge(loaded, 80)

                def fetch(b):
                    if not isinstance(b, int) or b > 0:
                        dve.wait_ge(convd, b * 3)
                    dve.tensor_copy(x[:, :], XT[:, b, :]).then_inc(x_in, 1)

                def exponents(b):
                    dve.wait_ge(q_proj, b + 1)
                    dve.tensor_scalar(neg[:, 0, :], ps_q[:, :], 0.0, None, ALU.min).then_inc(negged, 1)
                    dve.wait_ge(kv_proj, b + 1)
                    dve.wait_ge(v_out, b + 1)
                    dve.tensor_scalar(neg[:, 1, :].rearrange("p (t c) -> p t c", t=4), ps_kv[:, :, 0:DIM],
                                      0.0, None, ALU.min).then_inc(negged, 1)

                def convolve(b):
                    if not isinstance(b, int) or b > 0:
                        dve.wait_ge(mixed, b * 2)
                    dve.wait_ge(x_in, b + 1)
                    dve.tensor_scalar(conv[:, :], x[:, 0:N], vec[:, 0:1], vec[:, 3:4], ALU.mult, ALU.add).then_inc(convd, 1)
                    for k in (1, 2):
                        dve.wait_ge(convd, b * 3 + k)
                        dve.scalar_tensor_tensor(out=conv[:, :], in0=x[:, k:k + N], scalar=vec[:, k:k + 1], in1=conv[:, :],
                                                 op0=ALU.mult, op1=ALU.add).then_inc(convd, 1)

                def features(b):
                    dve.wait_ge(exped, b + 1)
                    dve.scalar_tensor_tensor(out=phi_k[:, :, :], in0=ps_kv[:, :, 0:DIM], scalar=0.0,
                                             in1=neg[:, 1, :].rearrange("p (t c) -> p t c", t=4),
                                             op0=ALU.max, op1=ALU.add).then_inc(phi, 1)
                    dve.scalar_tensor_tensor(out=phi_q[:, :], in0=ps_q[:, :], scalar=0.0, in1=neg[:, 0, :],
                                             op0=ALU.max, op1=ALU.add).then_inc(phi, 1)

                def front(b):
                    fetch(b)
                    exponents(b)
                    convolve(b)
                    features(b)

                def step(b, more=True):
                    if more:
                        fetch(b + 1)
                    dve.wait_ge(state, b + 1)
                    dve.tensor_scalar(ks[:, :], blocks[:, :], ps_state[:, DIM:DIM + 1], None, ALU.mult).then_inc(masked, 1)
                    dve.tensor_tensor(kv[:, :], blocks[:, :], ps_state[:, 0:DIM], ALU.mult).then_inc(masked, 1)
                    if more:
                        exponents(b + 1)
                    dve.wait_ge(nums, b * 2 + 1)
                    dve.tensor_scalar(den[:, :], ps_den[:, :], 1e-6, None, ALU.max).then_inc(capped, 1)
                    dve.wait_ge(recipd, b + 1)
                    dve.wait_ge(nums, b * 2 + 2)
                    if not isinstance(b, int) or b > 0:
                        dve.wait_ge(projected, b)
                    dve.tensor_tensor(mix[:, :], den[:, :], ps_num[:, :], ALU.mult).then_inc(mixed, 1)
                    dve.wait_ge(mixed, b * 2 + 1)
                    dve.wait_ge(convd, b * 3 + 3)
                    dve.tensor_tensor(mix[:, :], mix[:, :], conv[:, :], ALU.add).then_inc(mixed, 1)
                    if more:
                        convolve(b + 1)
                        features(b + 1)

                in_steps(dve, front, step)




def windowed_attention_stack(nc, w, XT):
    with ExitStack() as ctx:
        sb = lambda name, shape, dt=F32: ctx.enter_context(nc.sbuf_tensor(name, shape, dt))
        ps = lambda name, shape, dt=F32: ctx.enter_context(nc.psum_tensor(name, shape, dt))
        sem = lambda name: ctx.enter_context(nc.semaphore(name))

        w_qkv = sb("w_qkv", [P, 4, 768])
        w_o = sb("w_o", [P, 8, DIM])
        w_up = sb("w_up", [P, 2 * INNER2])
        w_down = sb("w_down", [P, 3, DIM])
        qk_gain = sb("qk_gain", [P, 4])
        ffn_vec = sb("ffn_vec", [P, 9])
        cos_t = sb("cos_t", [P, 2, N])
        sin_t = sb("sin_t", [P, 2, N])
        head_ones = sb("head_ones", [P, P])
        mean_ones = sb("mean_ones", [P, P])
        ident16 = sb("ident16", [P, P], BF16)
        mask16 = sb("mask16", [P, N], BF16)
        xs = sb("xs", [P, N])
        tab_c = sb("tab_c", [P, 2, 2, N])
        tab_s = sb("tab_s", [P, 2, 2, N])
        sq = sb("sq", [P, 2, 2, N])
        raw = sb("raw", [P, 3, 2, N])
        rn = sb("rn", [P, 2, N])
        qkn = sb("qkn", [P, 2, 2, N])
        qkc = sb("qkc", [P, 2, 2, N])
        qkr = sb("qkr", [P, 2, 2, N])
        pair = sb("pair", [P, 2, 2, 2, W + N])
        prob = sb("prob", [P, 16, 2, W])
        probT = sb("probT", [P, 16, 2, W])
        band = sb("band", [P, 2, 16, 5 * W])
        smax = sb("smax", [P, 16])
        ssum = sb("ssum", [P, 16])
        srec = sb("srec", [P, 16])
        v_sb = sb("v_sb", [P, 4, 4, 256])
        o_sb = sb("o_sb", [P, 8, N])
        x1 = sb("x1", [P, 1 + N])
        xs2 = sb("xs2", [P, N])
        cen = sb("cen", [P, N])
        cen2 = sb("cen2", [P, N])
        rstd = sb("rstd", [P, N])
        xn = cen2
        hid = sb("hid", [P, 3, N])
        eps_b = sb("eps_b", [P, 2])

        ps_qk = ps("ps_qk", [P, 2, N])
        ps_s = ps("ps_s", [P, 2, N])
        ps_n = ps("ps_n", [P, 2, N])
        ps_w = ps("ps_w", [P, 2, N])

        head_w = [sem(f"head_w{s}") for s in range(4)]
        gain_w = sem("gain_w")
        wo_w, up_w, down_w, vec_w = sem("wo_w"), sem("up_w"), sem("down_w"), sem("vec_w")
        const_w = sem("const_w")
        zeroed = sem("zeroed")
        xs_ready = sem("xs_ready")
        qk_proj = sem("qk_proj")
        squared = sem("squared")
        raw_out = sem("raw_out")
        sq_added = sem("sq_added")
        norm_summed = sem("norm_summed")
        norm_ln = sem("norm_ln")
        rnorm = sem("rnorm")
        tables = sem("tables")
        normed = sem("normed")
        turned = sem("turned")
        rotated = sem("rotated")
        paired = [sem("paired0"), sem("paired1")]
        scored = sem("scored")
        maxed = sem("maxed")
        shifted = sem("shifted")
        exped = sem("exped")
        summed = sem("summed")
        recipd = sem("recipd")
        scaled = sem("scaled")
        flipped = sem("flipped")
        banded = sem("banded")
        v_proj = sem("v_proj")
        v_out = sem("v_out")
        pv_done = sem("pv_done")
        o_out = sem("o_out")
        wo_done = sem("wo_done")
        x1_done = sem("x1_done")
        xs2_done = sem("xs2_done")
        mean_done = sem("mean_done")
        cen_done = sem("cen_done")
        cen2_done = sem("cen2_done")
        var_done = sem("var_done")
        var_ln = sem("var_ln")
        rstd_done = sem("rstd_done")
        xn_half = sem("xn_half")
        xn_done = sem("xn_done")
        up_done = sem("up_done")
        gelu_done = sem("gelu_done")
        hid_done = sem("hid_done")
        down_done = sem("down_done")
        x_done = sem("x_done")

        def live(i, s, lag):
            return not isinstance(i, int) or 0 <= 4 * i + s - lag < GROUPS

        def tail_live(i):
            return not isinstance(i, int) or 0 <= i - 2 < STEPS

        def upto(i, s, lag, per=1, part=None):
            part = per if part is None else part
            if isinstance(i, int):
                n = 4 * i + s - lag
                if n < 0:
                    return None
                if n >= GROUPS:
                    return per * GROUPS
                return per * n + part
            return i * (4 * per) + (per * (s - lag) + part)

        def step(i, lag, per=1, part=None):
            part = per if part is None else part
            if isinstance(i, int):
                k = i - lag
                if k < 0:
                    return None
                return per * min(k, STEPS - 1) + part if k < STEPS else per * STEPS
            return i * per + (part - per * lag)

        def wait(eng, s, value):
            if value is not None:
                eng.wait_ge(s, value)

        def layer_of(i, lag=0):
            return (i - lag) // 4 + 1 if isinstance(i, int) else ((i - lag) >> 2) + 1

        def run(eng, slots):
            for i in (0, 1):
                slots(i)
            with eng.Fori(2, STEPS) as i:
                slots(i)
            for i in (STEPS, STEPS + 1):
                slots(i)

        with nc.Block() as block:

            @block.sync
            def _(sp):
                def after(s, value):
                    if value is not None:
                        sp.wait_ge(s, value)
                        sp.wait_ge(zeroed, 4)

                def load_group(layer, s):
                    sp.dma_start(w_qkv[:, s, :], w["w_qkv"][layer, s]).then_inc(head_w[s], 16)

                def load_wo(layer, used=None):
                    after(wo_done, used)
                    sp.dma_start(w_o[:, :, :], w["w_o"][layer]).then_inc(wo_w, 16)

                def load_rest(layer, used=None):
                    after(up_done, None if used is None else used * 6)
                    sp.dma_start(w_up[:, :], w["w_up"][layer]).then_inc(up_w, 16)
                    after(x_done, None if used is None else used + B)
                    sp.dma_start(w_down[:, :, :], w["w_down"][layer]).then_inc(down_w, 16)
                    sp.dma_start(ffn_vec[:, :], w["ffn_vec"][layer]).then_inc(vec_w, 16)

                def load_gain(layer):
                    sp.dma_start(qk_gain[:, :], w["qk_gain"][layer]).then_inc(gain_w, 16)

                def pair_up(n, s):
                    par = s % 2
                    after(rotated, n + 1)
                    for h in range(4):
                        for half in range(2):
                            to = 64 * (h % 2) + 32 * half
                            sp.dma_start(pair[to:to + 32, par, :, h // 2, W:],
                                         qkr[32 * h:32 * h + 32, :, half, :]).then_inc(paired[par], 16)

                sp.wait_ge(zeroed, 4)
                load_group(0, 0)
                sp.dma_start(head_ones[:, :], w["head_ones"]).then_inc(const_w, 16)
                sp.dma_start(mean_ones[:, :], w["mean_ones"]).then_inc(const_w, 16)
                sp.dma_start(ident16[:, :], w["ident16"]).then_inc(const_w, 16)
                sp.dma_start(mask16[:, :], w["mask16"]).then_inc(const_w, 16)
                sp.dma_start(cos_t[:, :, :], w["cos_t"]).then_inc(const_w, 16)
                sp.dma_start(sin_t[:, :, :], w["sin_t"]).then_inc(const_w, 16)
                load_gain(0)
                for s in range(1, 4):
                    load_group(0, s)
                load_wo(0)
                load_rest(0)

                def layer_steps(layer):
                    for b in range(4):
                        i = layer * 4 + b
                        for s in range(4):
                            if not isinstance(layer, int) or i + s > 0:
                                pair_up(i * 4 + (s - 1), s - 1)
                            if b == 1 and s == 2 and (not isinstance(layer, int) or layer > 0):
                                load_wo(layer, layer * 4)
                            if b == 3 and (not isinstance(layer, int) or layer < DEPTH - 1):
                                after(v_proj, i * 8 + (2 * s + 2))
                                load_group(layer + 1, s)
                                if s == 3:
                                    after(tables, i + 1)
                                    load_gain(layer + 1)
                        if b == 1 and (not isinstance(layer, int) or layer > 0):
                            load_rest(layer, layer * 4)

                layer_steps(0)
                with sp.Fori(1, DEPTH - 1) as layer:
                    layer_steps(layer)
                layer_steps(DEPTH - 1)
                pair_up(GROUPS - 1, 3)
                sp.wait_ge(x_done, B + STEPS)

            @block.tensor
            def _(pe):
                pe.wait_ge(const_w, 96)

                def project_qk(i, s, x):
                    if x:
                        wait(pe, raw_out, upto(i, s, 0, 2, 1))
                    else:
                        if s == 0:
                            wait(pe, xs_ready, step(i, 0))
                        pe.wait_ge(head_w[s], layer_of(i) * 16)
                        wait(pe, raw_out, upto(i, s, 1, 2))
                    for half in range(2):
                        c = (2 * x + half) * P
                        mm = pe.matmul(ps_qk[:, half, :], w_qkv[:, s, c:c + P], xs[:, :], start=True, stop=True)
                    mm.then_inc(qk_proj, 1)

                def project_v(i, s):
                    wait(pe, v_out, upto(i, s, 1, 2))
                    last = (x1_done, cen_done, var_ln, hid_done)[s]
                    wait(pe, last, step(i, 2, 3) if s == 3 else step(i, 2))
                    for k in range(2):
                        for t in (2 * k, 2 * k + 1):
                            mm = pe.matmul(ps_w[:, k, (t % 2) * 256:(t % 2) * 256 + 256],
                                           xs[:, t * P:t * P + P], w_qkv[:, s, 512:768],
                                           start=(t % 2 == 0), stop=True, skip_group_check=True)
                        mm.then_inc(v_proj, 1)

                def sum_norms(i, s):
                    for x in range(2):
                        wait(pe, sq_added, upto(i, s, 0, 2, x + 1))
                        wait(pe, o_out, upto(i, s, 4, 2, x + 1))
                        pe.matmul(ps_n[:, x, :], head_ones[:, :], sq[:, x, 0, :],
                                  start=True, stop=True).then_inc(norm_summed, 1)

                def score(i, s):
                    par = s % 2
                    wait(pe, shifted, upto(i, s, 3))
                    if isinstance(i, int):
                        pe.wait_ge(paired[par], 128 * ((4 * i + s - 2) // 2 + 1))
                    else:
                        pe.wait_ge(paired[par], i * 256 + 128 * ((s - 2) // 2 + 1))
                    for e in range(2):
                        pe.matmul(ps_s[:, e, :], ident16[:, :], mask16[:, :], start=True, stop=False,
                                  skip_group_check=True)
                    for t in range(4):
                        for p in range(2):
                            for wd in range(4):
                                for e in range(2):
                                    r = slice(64 * e, 64 * e + 64)
                                    tok = P * t + W * wd
                                    c = (2 * t + p) * 2 * W
                                    mm = pe.matmul(ps_s[W * wd:W * wd + W, e, c:c + 2 * W],
                                                   pair[r, par, 0, p, W + tok:2 * W + tok],
                                                   pair[r, par, 1, p, tok:tok + 2 * W],
                                                   start=False, stop=True, skip_group_check=True)
                    mm.then_inc(scored, 1)

                def values(i, s):
                    par = s % 2
                    wait(pe, banded, upto(i, s, 4))
                    wait(pe, norm_ln, upto(i, s, 1))
                    wait(pe, o_out, upto(i, s, 5, 2))
                    for p in range(2):
                        for t in range(4):
                            width = min(5 * W, N - P * t)
                            for e in range(2):
                                mm = pe.matmul(ps_n[64 * e:64 * e + 64, p, P * t:P * t + width],
                                               v_sb[:, s, t, (2 * p + e) * 64:(2 * p + e) * 64 + 64],
                                               band[:, par, e * 8 + 2 * t + p, 0:width],
                                               start=(t == 0), stop=(t == 3), skip_group_check=True)
                        mm.then_inc(pv_done, 1)

                def attn_out(i):
                    wait(pe, o_out, upto(i, 0, 5, 2))
                    pe.wait_ge(wo_w, layer_of(i, 2) * 16)
                    wait(pe, v_out, upto(i, 0, 1, 2))
                    before = step(i, 3)
                    wait(pe, x_done, None if before is None else before + B)
                    for c in range(8):
                        mm = pe.matmul(ps_w[:, 0, :], w_o[:, c, :], o_sb[:, c, :], start=(c == 0), stop=(c == 7))
                    mm.then_inc(wo_done, 1)

                def mean(i):
                    wait(pe, xs2_done, step(i, 2))
                    wait(pe, v_out, upto(i, 1, 1, 2))
                    pe.matmul(ps_w[:, 0, :], mean_ones[:, :], xs2[:, :], start=True, stop=True).then_inc(mean_done, 1)

                def variance(i):
                    wait(pe, cen2_done, step(i, 2))
                    wait(pe, v_out, upto(i, 1, 0, 2))
                    pe.matmul(ps_w[:, 0, :], mean_ones[:, :], cen2[:, :], start=True, stop=True).then_inc(var_done, 1)

                def up(i, chunks):
                    if 0 in chunks:
                        wait(pe, xn_done, step(i, 2))
                        pe.wait_ge(up_w, layer_of(i, 2) * 16)
                        wait(pe, v_out, upto(i, 2, 0, 2))
                    for k in chunks:
                        gate, c = ((1, 0), (1, 1), (0, 0), (0, 1), (1, 2), (0, 2))[k]
                        m = min(P, INNER2 - P * c)
                        if k in (2, 3):
                            wait(pe, gelu_done, step(i, 2, 3, k - 1))
                        elif k in (4, 5):
                            wait(pe, hid_done, step(i, 2, 3, k - 3))
                        f = gate * INNER2 + P * c
                        pe.matmul(ps_w[0:m, k % 2, :], w_up[:, f:f + m], xn[:, :],
                                  start=True, stop=True).then_inc(up_done, 1)

                def down(i):
                    wait(pe, hid_done, step(i, 2, 3))
                    pe.wait_ge(down_w, layer_of(i, 2) * 16)
                    wait(pe, v_out, upto(i, 3, 0, 2))
                    for c in range(3):
                        m = min(P, INNER2 - P * c)
                        mm = pe.matmul(ps_w[:, 0, :], w_down[0:m, c, :], hid[0:m, c, :], start=(c == 0), stop=(c == 2))
                    mm.then_inc(down_done, 1)

                def slots(i):
                    for s in range(4):
                        tail = tail_live(i)
                        if tail and s == 0:
                            attn_out(i)
                        if tail and s == 1:
                            mean(i)
                        if live(i, s, 0):
                            project_qk(i, s, 0)
                        if tail and s == 3:
                            up(i, (2, 3))
                        if live(i, s, 4):
                            values(i, s)
                        if tail and s == 3:
                            up(i, (4, 5))
                        if live(i, s, 0):
                            project_qk(i, s, 1)
                            project_v(i, s)
                        if live(i, s, 2):
                            score(i, s)
                        if live(i, s, 0):
                            sum_norms(i, s)
                        if tail and s == 1:
                            variance(i)
                        if tail and s == 2:
                            up(i, (0, 1))
                        if tail and s == 3:
                            down(i)

                run(pe, slots)

            @block.scalar
            def _(act):
                act.wait_ge(zeroed, 4)

                def shift_in(i, step_index):
                    b = i % 4 if isinstance(i, int) else i & 3
                    act.wait_ge(x_done, i + 1)
                    if not isinstance(i, int) or i > 0:
                        act.wait_ge(v_proj, i * 8)
                    act.activation(xs[0:64, :], XT[0:64, b, 1:1 + N], ACT.Copy)
                    act.activation(xs[64:128, :], XT[64:128, b, 0:N], ACT.Copy).then_inc(xs_ready, 1)

                def squares(i, s, x):
                    wait(act, norm_summed, upto(i, s, 1, 2, x + 1))
                    wait(act, qk_proj, upto(i, s, 0, 2, x + 1))
                    act.activation(sq[:, x, :, :], ps_qk[:, :, :], ACT.Square).then_inc(squared, 1)
                    wait(act, normed, upto(i, s, 1, 2) if x else upto(i, s, 2, 2, 1))
                    act.activation(raw[:, 2 if x else s % 2, :, :], ps_qk[:, :, :], ACT.Copy).then_inc(raw_out, 1)

                def values_out(i, s):
                    if s == 0:
                        wait(act, wo_done, step(i, 2))
                    for p in range(2):
                        wait(act, pv_done, upto(i, s, 4, 2, p + 1))
                        act.activation(o_sb[:, 2 * s + p, :], ps_n[:, p, :], ACT.Copy).then_inc(o_out, 1)

                def rnorms(i, s):
                    wait(act, norm_summed, upto(i, s, 0, 2))
                    wait(act, normed, upto(i, s, 1, 2))
                    act.activation(rn[:, :, :], ps_n[:, :, :], ACT.Ln, bias=eps_b[:, 0:1], scale=2.0 ** 32).then_inc(norm_ln, 1)
                    wait(act, norm_ln, upto(i, s, 0))
                    act.activation(rn[:, :, :], rn[:, :, :], ACT.Exp, scale=-0.5).then_inc(rnorm, 1)

                def exps(i, s):
                    wait(act, shifted, upto(i, s, 2))
                    act.activation(prob[:, :, :, :], prob[:, :, :, :], ACT.Exp).then_inc(exped, 1)

                def bands(i, s):
                    par = (s - 3) % 2
                    wait(act, flipped, upto(i, s, 3))
                    wait(act, pv_done, upto(i, s, 5, 2))
                    for wd in range(4):
                        rows = slice(W * wd, W * wd + W)
                        act.activation(band[rows, par, :, W * wd:W * wd + W], probT[rows, :, 1, :], ACT.Copy)
                        if wd:
                            before = slice(W * wd - W, W * wd)
                            act.activation(band[before, par, :, W * wd:W * wd + W], probT[rows, :, 0, :], ACT.Copy)
                    heads = lambda view: view.rearrange("p (e c) k -> p e c k", e=2)
                    act.activation(heads(band[96:128, par, :, 4 * W:5 * W])[:, :, 0:6, :],
                                   heads(probT[0:32, :, 0, :])[:, :, 2:8, :], ACT.Copy).then_inc(banded, 1)

                def shift_mid(i):
                    wait(act, x1_done, step(i, 2))
                    act.activation(xs2[0:64, :], x1[0:64, 1:1 + N], ACT.Copy)
                    act.activation(xs2[64:128, :], x1[64:128, 0:N], ACT.Copy).then_inc(xs2_done, 1)

                def centred_square(i):
                    wait(act, cen_done, step(i, 2))
                    wait(act, up_done, step(i, 3, 6))
                    act.activation(cen2[:, :], cen[:, :], ACT.Square).then_inc(cen2_done, 1)

                def rstds(i):
                    wait(act, var_done, step(i, 2))
                    act.activation(rstd[:, :], ps_w[:, 0, :], ACT.Ln, bias=eps_b[:, 1:2]).then_inc(var_ln, 1)
                    wait(act, var_ln, step(i, 2))
                    act.activation(rstd[:, :], rstd[:, :], ACT.Exp, scale=-0.5).then_inc(rstd_done, 1)

                def gelus(i, chunks):
                    pe_chunk = (0, 1, 4)
                    for c in chunks:
                        m = min(P, INNER2 - P * c)
                        wait(act, up_done, step(i, 2, 6, pe_chunk[c] + 1))
                        act.activation(hid[0:m, c, :], ps_w[0:m, pe_chunk[c] % 2, :], ACT.Gelu,
                                       bias=ffn_vec[0:m, 5 + c:6 + c]).then_inc(gelu_done, 1)

                def slots(i):
                    tail = tail_live(i)
                    for s in range(4):
                        if s == 0 and live(i, 0, 0):
                            shift_in(i, i)
                        if live(i, s, 0):
                            squares(i, s, 0)
                        if live(i, s, 4):
                            values_out(i, s)
                        if tail and s == 3:
                            gelus(i, (2,))
                            act.preload_act_table_set("natural_log_exp_and_others")
                        if live(i, s, 0):
                            squares(i, s, 1)
                        if tail and s == 0:
                            shift_mid(i)
                        if tail and s == 1:
                            centred_square(i)
                        if live(i, s, 3):
                            bands(i, s)
                        if live(i, s, 0):
                            rnorms(i, s)
                        if live(i, s, 2):
                            exps(i, s)
                        if tail and s == 1:
                            rstds(i)
                        if tail and s == 2:
                            wait(act, vec_w, layer_of(i, 2) * 16)
                            gelus(i, (0, 1))

                act.preload_act_table_set("natural_log_exp_and_others")
                run(act, slots)

            @block.vector
            def _(dve):
                dve.memset(pair[:, :, :, :, 0:W], 0.0).then_inc(zeroed, 1)
                dve.memset(x1[:, 0:1], 0.0).then_inc(zeroed, 1)
                dve.memset(eps_b[:, 1:2], LN_EPS).then_inc(x_done, B)
                dve.memset(eps_b[:, 0:1], 2.0 ** -62).then_inc(zeroed, 1)
                dve.memset(band[:, :, :, :], 0.0).then_inc(zeroed, 1)
                dve.wait_ge(zeroed, 4)

                def normalise(i, s):
                    wait(dve, rotated, upto(i, s, 2))
                    wait(dve, rnorm, upto(i, s, 1))
                    for x in range(2):
                        r = rn[:, x:x + 1, :].broadcast_to([P, 2, N])
                        dve.scalar_tensor_tensor(out=qkn[:, x, :, :], in0=r, scalar=RN_CAP, in1=raw[:, 2 if x else (s - 1) % 2, :, :],
                                                 op0=ALU.min, op1=ALU.mult).then_inc(normed, 1)

                def turn(i, s, sine):
                    flat = lambda a: a[:, :, :, :].rearrange("p x h n -> p (x h n)")
                    if not sine:
                        wait(dve, normed, upto(i, s, 1, 2))
                        if (s - 1) % 4 == 0:
                            wait(dve, tables, step(i, 0))
                    table, product = (tab_s, qkn) if sine else (tab_c, qkc)
                    dve.tensor_tensor(flat(product), flat(qkn), flat(table), ALU.mult).then_inc(turned, 1)

                def v_copy(i, s):
                    for k in range(2):
                        wait(dve, v_proj, upto(i, s, 0, 2, k + 1))
                        dve.tensor_copy(v_sb[:, s, 2 * k:2 * k + 2, :], ps_w[:, k, :]).then_inc(v_out, 1)

                def maxima(i, s):
                    wait(dve, scored, upto(i, s, 2))
                    view = ps_s[:, :, :].rearrange("p e (c k) -> p (e c) k", k=2 * W)
                    dve.tensor_reduce(smax[:, :], view, AX.X, ALU.max).then_inc(maxed, 1)
                    wait(dve, maxed, upto(i, s, 2))
                    wait(dve, flipped, upto(i, s, 3))
                    dve.tensor_tensor(prob[:, :, :, :].rearrange("p c w k -> p c (w k)"), view,
                                      smax[:, :].unsqueeze(2).broadcast_to([P, 16, 2 * W]),
                                      ALU.subtract).then_inc(shifted, 1)

                def sums(i, s):
                    wait(dve, exped, upto(i, s, 3))
                    dve.tensor_reduce(ssum[:, :], prob[:, :, :, :].rearrange("p c w k -> p c (w k)"), AX.X, ALU.add).then_inc(summed, 1)
                    wait(dve, summed, upto(i, s, 3))
                    wait(dve, scaled, upto(i, s, 4))
                    dve.reciprocal(srec[:, :], ssum[:, :]).then_inc(recipd, 1)

                def flip(i, s):
                    wait(dve, scaled, upto(i, s, 3))
                    wait(dve, banded, upto(i, s, 4))
                    dve.transpose(probT[:, :, :, :].rearrange("p c w k -> p (c w k)"),
                                  prob[:, :, :, :].rearrange("p c w k -> p (c w k)")).then_inc(flipped, 1)

                def hidden(i, c):
                    k = (2, 3, 5)[c]
                    m = min(P, INNER2 - P * c)
                    wait(dve, up_done, step(i, 2, 6, k + 1))
                    wait(dve, gelu_done, step(i, 2, 3, c + 1))
                    dve.scalar_tensor_tensor(out=hid[0:m, c, :], in0=ps_w[0:m, k % 2, :],
                                             scalar=ffn_vec[0:m, 2 + c:3 + c], in1=hid[0:m, c, :],
                                             op0=ALU.add, op1=ALU.mult).then_inc(hid_done, 1)

                def slots(i):
                    tail = tail_live(i)
                    for s in range(4):
                        bj = (i - 2) % 4 if isinstance(i, int) else (i - 2) & 3
                        if live(i, s, 1):
                            normalise(i, s)
                        if tail and s == 0:
                            wait(dve, wo_done, step(i, 2))
                            dve.tensor_tensor(x1[:, 1:1 + N], XT[:, bj, 1:1 + N], ps_w[:, 0, :], ALU.add).then_inc(x1_done, 1)
                        if tail and s == 1:
                            wait(dve, mean_done, step(i, 2))
                            dve.tensor_tensor(cen[:, :], xs2[:, :], ps_w[:, 0, :], ALU.subtract).then_inc(cen_done, 1)
                        if tail and s == 2:
                            wait(dve, rstd_done, step(i, 2))
                            dve.wait_ge(vec_w, layer_of(i, 2) * 16)
                            dve.scalar_tensor_tensor(out=xn[:, :], in0=cen[:, :], scalar=ffn_vec[:, 0:1], in1=rstd[:, :],
                                                     op0=ALU.mult, op1=ALU.mult).then_inc(xn_half, 1)
                            wait(dve, xn_half, step(i, 2))
                            dve.tensor_scalar(xn[:, :], xn[:, :], ffn_vec[:, 1:2], None, ALU.add).then_inc(xn_done, 1)
                        if tail and s == 3:
                            hidden(i, 0)
                            hidden(i, 1)
                        if live(i, s, 3):
                            sums(i, s)
                        if tail and s == 3:
                            hidden(i, 2)
                        if live(i, s, 1):
                            turn(i, s, False)
                        if live(i, s, 3):
                            flip(i, s)
                        if live(i, s, 1):
                            turn(i, s, True)
                        if live(i, s, 0):
                            v_copy(i, s)
                        if live(i, s, 2):
                            maxima(i, s)
                        if tail and s == 3:
                            wait(dve, down_done, step(i, 2))
                            dve.scalar_tensor_tensor(out=XT[:, bj, 1:1 + N], in0=ps_w[:, 0, :], scalar=ffn_vec[:, 8:9],
                                                     in1=x1[:, 1:1 + N], op0=ALU.add, op1=ALU.add).then_inc(x_done, 1)

                run(dve, slots)

            @block.gpsimd
            def _(pool):
                pool.wait_ge(const_w, 96)

                def make_tables(i):
                    for x in range(2):
                        for half in range(2):
                            g = qk_gain[:, 2 * x + half:2 * x + half + 1]
                            pool.tensor_scalar(tab_c[:, x, half, :], cos_t[:, x, :], g, 1.0, ALU.mult, ALU.mult)
                            last = pool.tensor_scalar(tab_s[:, x, half, :], sin_t[:, x, :], g,
                                                      -1.0 if half else 1.0, ALU.mult, ALU.mult)
                    last.then_inc(tables, 1)

                def add_squares(i, s):
                    wait(pool, norm_summed, upto(i, s, 1, 2))
                    for x in range(2):
                        wait(pool, squared, upto(i, s, 0, 2, x + 1))
                        pool.tensor_tensor(sq[:, x, 0, :], sq[:, x, 0, :], sq[:, x, 1, :], ALU.add).then_inc(sq_added, 1)

                def add_turned(i, s):
                    wait(pool, turned, upto(i, s, 1, 2))
                    wait(pool, scored, upto(i, s, 3))
                    if isinstance(i, int):
                        if 4 * i + s >= 2:
                            pool.wait_ge(paired[s % 2], 128 * ((4 * i + s - 2) // 2 + 1))
                    else:
                        pool.wait_ge(paired[s % 2], i * 256 + 128 * ((s - 2) // 2 + 1))
                    pool.tensor_tensor(qkr[:, :, 0, :], qkc[:, :, 0, :], qkn[:, :, 1, :], ALU.add)
                    pool.tensor_tensor(qkr[:, :, 1, :], qkc[:, :, 1, :], qkn[:, :, 0, :], ALU.add).then_inc(rotated, 1)

                def scale_probs(i, s):
                    wait(pool, recipd, upto(i, s, 3))
                    view = prob[:, :, :, :].rearrange("p c w k -> p c (w k)")
                    pool.tensor_tensor(view, view, srec[:, :].unsqueeze(2).broadcast_to([P, 16, 2 * W]),
                                       ALU.mult).then_inc(scaled, 1)

                def slots(i):
                    for s in range(4):
                        if live(i, s, 3):
                            scale_probs(i, s)
                        if live(i, s, 0):
                            add_squares(i, s)
                        if s == 0 and live(i, 0, 0):
                            pool.wait_ge(gain_w, layer_of(i) * 16)
                        if live(i, s, 1):
                            add_turned(i, s)
                        if s == 0 and live(i, 0, 0):
                            make_tables(i)

                run(pool, slots)


def power_attention(nc, w, XT, YT):
    with ExitStack() as ctx:
        sb = lambda name, shape, dt=F32: ctx.enter_context(nc.sbuf_tensor("pa_" + name, shape, dt))
        ps = lambda name, shape, dt=F32: ctx.enter_context(nc.psum_tensor("pa_" + name, shape, dt))
        sem = lambda name: ctx.enter_context(nc.semaphore("pa_" + name))
        wq, wk = sb("wq", [P, 16, 32]), sb("wk", [P, 16, 32])
        wv = sb("wv", [P, DIM])
        wo = sb("wo", [P, 4, DIM])
        dist = sb("dist", [P, N])
        slopes, power = sb("slopes", [P, 16]), sb("power", [P, 1])
        cst = sb("cst", [P, 4])
        row8 = sb("row8", [P, P])
        tick = sb("tick", [P, 16])
        eps6 = sb("eps6", [P, 1])
        x = sb("x", [P, N])
        v_pad = sb("v_pad", [P, 4, 16, 32])
        qT, kT = sb("qT", [P, 2, N]), sb("kT", [P, 2, N])
        z = sb("z", [P, 4, 4, N])
        a = sb("a", [P, 4, 4, N])
        pk = sb("pk", [P, 4, 4, N])
        masked_w = sb("masked_w", [P, 3 * P])
        rd, o_raw = sb("rd", [P, N]), sb("o_raw", [P, N])
        oT = sb("oT", [P, 4, N])
        ps_s = ps("ps_s", [P, 4, N])
        ps_p = ps("ps_p", [P, N])
        ps_o = ps("ps_o", [P, 2, N])
        ps_d = ps("ps_d", [P, N])
        names = ("loaded", "zeroed", "filled", "set_up", "x_in", "v_proj", "v_out", "q_proj", "k_proj", "q_out", "k_out",
                 "scored", "zd", "masked", "relud", "absd", "lned", "subd", "exped", "valued", "capped", "o_copied",
                 "den_ln", "den_r", "spread", "o_out", "projected", "y_out")
        (loaded, zeroed, filled, set_up, x_in, v_proj, v_out, q_proj, k_proj, q_out, k_out,
         scored, zd, masked, relud, absd, lned, subd, exped, valued, capped, o_copied,
         den_ln, den_r, spread, o_out, projected, y_out) = map(sem, names)
        UNITS = 16

        def live(b, u):
            return not isinstance(b, int) or 0 <= UNITS * b + u < UNITS * B

        def live_group(b, g):
            return live(b, 4 * g)

        def unit_wait(eng, s, b, u, per=1, part=None):
            part = per if part is None else part
            if live(b, u):
                eng.wait_ge(s, b * (UNITS * per) + (per * u + part))

        def group_wait(eng, s, b, g):
            if not isinstance(b, int) or 4 * b + g >= 0:
                eng.wait_ge(s, b * 4 + (g + 1))

        def over_slots(eng, slot):
            for u in range(UNITS):
                slot(0, u)
            with eng.Fori(1, B) as b:
                for u in range(UNITS):
                    slot(b, u)
            for u in range(10):
                slot(B, u)

        with nc.Block() as block:

            @block.sync
            def _(sp):
                sp.wait_ge(zeroed, 3)
                with nc.allow_non_contiguous_dma(reason="32-byte runs of head columns, once"):
                    sp.dma_start(wq[:, :, 0:8], w["pa_wq"].rearrange("c (h d) -> c h d", d=8)).then_inc(loaded, 16)
                    sp.dma_start(wk[:, :, 0:8], w["pa_wk"].rearrange("c (h d) -> c h d", d=8)).then_inc(loaded, 16)
                    for c in range(4):
                        sp.dma_start(wo[32 * c:32 * c + 8, :, :],
                                     w["pa_wo"].rearrange("(g c d) o -> c d g o", c=4, d=8)[c]).then_inc(loaded, 16)
                sp.dma_start(wv[:, :], w["pa_wv"]).then_inc(loaded, 16)
                sp.dma_start(dist[:, :], w["pa_dist"]).then_inc(loaded, 16)
                sp.dma_start(slopes[:, :], w["pa_slopes"]).then_inc(loaded, 16)
                sp.dma_start(power[:, :], w["pa_power"]).then_inc(loaded, 16)
                sp.dma_start(row8[:, :], w["pa_row8"]).then_inc(loaded, 16)

            @block.tensor
            def _(pe):
                pe.wait_ge(loaded, 176)
                pe.wait_ge(set_up, 3)

                def project_q(b, g):
                    if g in (0, 4):
                        pe.wait_ge(x_in, b + 1 + g // 4)
                    group_wait(pe, k_out, b, g - 1)
                    pe.matmul(ps_p[:, :], wq[:, 4 * (g % 4):4 * (g % 4) + 4, :].rearrange("c h d -> c (h d)"), x[:, :],
                              start=True, stop=True).then_inc(q_proj, 1)

                def project_k(b, g):
                    group_wait(pe, q_out, b, g)
                    pe.matmul(ps_p[:, :], wk[:, 4 * (g % 4):4 * (g % 4) + 4, :].rearrange("c h d -> c (h d)"), x[:, :],
                              start=True, stop=True).then_inc(k_proj, 1)

                def project_v(b):
                    group_wait(pe, o_out, b, -2)
                    for t in range(4):
                        mm = pe.matmul(ps_d[:, P * t:P * t + P], x[:, P * t:P * t + P], wv[:, :],
                                       start=(t == 0), stop=True, skip_group_check=True)
                    mm.then_inc(v_proj, 1)

                def score(b, u):
                    g, kt = u // 4, u % 4
                    n = N - P * kt
                    if kt == 0:
                        group_wait(pe, k_out, b, g)
                    for c in range(4):
                        r = slice(32 * c, 32 * c + 32)
                        unit_wait(pe, zd, b, u - 1, 4, c + 1)
                        pe.matmul(ps_s[:, c, 0:n], kT[r, g % 2, P * kt:P * kt + P], qT[r, g % 2, P * kt:N],
                                  start=True, stop=True).then_inc(scored, 1)

                def values(b, u):
                    g, kt = (u // 4) % 4, u % 4
                    unit_wait(pe, exped, b, u)
                    if kt == 0:
                        group_wait(pe, o_copied, b, u // 4 - 2)
                        group_wait(pe, capped, b, u // 4 - 2)
                    if u == 0:
                        pe.wait_ge(v_out, b + 1)
                    bank = ps_o[:, g % 2, :]
                    for c in range(4):
                        mm = pe.matmul(bank[32 * c:32 * c + 32, P * kt:N], v_pad[:, kt, 4 * g + c, :],
                                       pk[:, kt, c, 0:N - P * kt], start=(kt == 0), stop=True, skip_group_check=True)
                    if kt:
                        mm = pe.matmul(bank[:, 0:P * kt], v_pad[:, kt, 4 * g:4 * g + 4, :].rearrange("p c d -> p (c d)"),
                                       masked_w[:, 0:P * kt], start=False, stop=True, skip_group_check=True)
                    mm.then_inc(valued, 1)

                def spread_denominators(b, g):
                    group_wait(pe, den_r, b, g)
                    group_wait(pe, o_out, b, g - 1)
                    if g == 0 and not isinstance(b, int):
                        pe.wait_ge(y_out, b)
                    if g == -1 and (not isinstance(b, int) or b < B):
                        pe.wait_ge(v_out, b + 1)
                    pe.matmul(ps_d[:, :], row8[:, :], rd[:, :], start=True, stop=True).then_inc(spread, 1)

                def project_out(b):
                    group_wait(pe, o_out, b, -1)
                    for g in range(4):
                        mm = pe.matmul(ps_d[:, :], wo[:, g, :], oT[:, g, :], start=(g == 0), stop=(g == 3))
                    mm.then_inc(projected, 1)

                def slot(b, u):
                    if live(b, u):
                        score(b, u)
                        if u % 4 == 0:
                            project_q(b, (u + 4) // 4)
                        if u % 4 == 2:
                            project_k(b, (u + 2) // 4)
                        if u == 3:
                            project_v(b)
                    if u % 4 == 1 and live_group(b, (u - 9) // 4):
                        spread_denominators(b, (u - 9) // 4)
                    if u == 7 and live_group(b, -1):
                        project_out(b)
                    if live(b, u - 4):
                        values(b, u - 4)

                project_q(0, 0)
                project_k(0, 0)
                over_slots(pe, slot)

            @block.scalar
            def _(act):
                act.wait_ge(set_up, 1)
                act.wait_ge(loaded, 176)
                act.activation(cst[:, 1:2], cst[:, 1:2], ACT.Ln, bias=1.0).then_inc(filled, 1)
                act.wait_ge(filled, 1)
                act.wait_ge(set_up, 2)
                act.activation(cst[:, 2:3], cst[:, 1:2], ACT.Exp, bias=cst[:, 0:1], scale=cst[:, 3:4]).then_inc(filled, 1)

                def q_copy(b, g):
                    group_wait(act, q_proj, b, g)
                    if g >= 2 or not isinstance(b, int):
                        act.wait_ge(scored, b * 64 + (16 * g - 16))
                    act.activation(qT[:, g % 2, :], ps_p[:, :], ACT.Copy, scale=16.0 / 8.0 ** 0.5).then_inc(q_out, 1)

                def k_copy(b, g):
                    group_wait(act, k_proj, b, g)
                    act.activation(kT[:, g % 2, :], ps_p[:, :], ACT.Copy).then_inc(k_out, 1)

                def v_copy(b):
                    act.wait_ge(v_proj, b + 1)
                    unit_wait(act, valued, b, -1)
                    act.activation(v_pad[:, :, :, 0:8],
                                   ps_d[:, :].rearrange("p (t h d) -> p t h d", t=4, d=8), ACT.Copy).then_inc(v_out, 1)

                def logs(b, u):
                    n, ring = N - P * (u % 4), u % 4
                    unit_wait(act, absd, b, u)
                    act.activation(a[:, ring, :, 0:n], a[:, ring, :, 0:n], ACT.Ln, bias=1.0)
                    act.activation(z[:, ring, :, 0:n], z[:, ring, :, 0:n], ACT.Ln, bias=1.0).then_inc(lned, 1)

                def weights(b, u):
                    n, ring = N - P * (u % 4), u % 4
                    unit_wait(act, subd, b, u)
                    unit_wait(act, valued, b, u - 4)
                    act.activation(pk[:, ring, :, 0:n], z[:, ring, :, 0:n], ACT.Exp,
                                   bias=cst[:, 0:1], scale=power[:, 0:1]).then_inc(exped, 1)

                def sums_out(b, g):
                    group_wait(act, capped, b, g)
                    group_wait(act, o_out, b, g - 1)
                    act.activation(o_raw[:, :], ps_o[:, g % 2, :], ACT.Copy).then_inc(o_copied, 1)
                    act.activation(rd[:, :], rd[:, :], ACT.Ln).then_inc(den_ln, 1)
                    group_wait(act, den_ln, b, g)
                    act.activation(rd[:, :], rd[:, :], ACT.Exp, scale=-1.0).then_inc(den_r, 1)

                def slot(b, u):
                    if live(b, u):
                        if u % 4 == 1:
                            q_copy(b, (u + 3) // 4)
                        if u % 4 == 3:
                            k_copy(b, (u + 1) // 4)
                        if u == 4:
                            v_copy(b)
                    if u % 4 == 0 and live_group(b, (u - 8) // 4):
                        sums_out(b, (u - 8) // 4)
                    if u == 8 and live_group(b, -1):
                        act.wait_ge(projected, b)
                        act.activation(YT[:, b - 1, 1:1 + N], ps_d[:, :], ACT.Copy).then_inc(y_out, 1)
                    if live(b, u - 3):
                        weights(b, u - 3)
                    if live(b, u - 1):
                        logs(b, u - 1)

                q_copy(0, 0)
                k_copy(0, 0)
                over_slots(act, slot)

            @block.vector
            def _(dve):
                dve.memset(wq[:, :, :], 0.0).then_inc(zeroed, 1)
                dve.memset(wk[:, :, :], 0.0).then_inc(zeroed, 1)
                dve.memset(wo[:, :, :], 0.0).then_inc(zeroed, 1)
                dve.memset(v_pad[:, :, :, :], 0.0).then_inc(zeroed, 1)
                dve.memset(masked_w[:, :], 1.0).then_inc(zeroed, 1)
                dve.memset(cst[:, 1:2], 10000.0).then_inc(set_up, 1)
                dve.wait_ge(zeroed, 5)
                dve.memset(v_pad[:, :, :, 8:9], 1.0)
                dve.tensor_copy(x[:, :], XT[:, 0, 1:1 + N]).then_inc(x_in, 1)
                dve.wait_ge(loaded, 176)
                dve.tensor_scalar(cst[:, 0:1], power[:, :], -float(np.log(2.0)), None, ALU.mult)
                dve.tensor_scalar(cst[:, 3:4], power[:, :], -1.0, None, ALU.mult).then_inc(set_up, 1)
                dve.wait_ge(filled, 2)
                dve.tensor_scalar(masked_w[:, :], masked_w[:, :], cst[:, 2:3], None, ALU.mult).then_inc(set_up, 1)

                def cap(b, g):
                    unit_wait(dve, valued, b, 4 * g + 3)
                    group_wait(dve, spread, b, g - 1)
                    dve.tensor_scalar(rd[:, :], ps_o[:, g % 2, :], 1e-6, 1e-30, ALU.add, ALU.max).then_inc(capped, 1)

                def negated(b, u):
                    g, n, ring = u // 4, N - P * (u % 4), u % 4
                    unit_wait(dve, exped, b, u - 4)
                    for c in range(4):
                        unit_wait(dve, scored, b, u, 4, c + 1)
                        dve.scalar_tensor_tensor(out=z[:, ring, c, 0:n], in0=dist[:, 0:n], scalar=slopes[:, 4 * g + c:4 * g + c + 1],
                                                 in1=ps_s[:, c, 0:n], op0=ALU.mult, op1=ALU.subtract).then_inc(zd, 1)

                def parts(b, u):
                    n, ring = N - P * (u % 4), u % 4
                    unit_wait(dve, masked, b, u)
                    dve.tensor_scalar(a[:, ring, :, 0:n], z[:, ring, :, 0:n], -2.0, 0.0, ALU.mult, ALU.max).then_inc(relud, 1)
                    unit_wait(dve, relud, b, u)
                    dve.tensor_tensor(z[:, ring, :, 0:n], z[:, ring, :, 0:n], a[:, ring, :, 0:n], ALU.add).then_inc(absd, 1)

                def heads_out(b, g):
                    group_wait(dve, spread, b, g)
                    if g == 0 and not isinstance(b, int):
                        dve.wait_ge(projected, b)
                    dve.tensor_tensor(oT[:, g % 4, :], o_raw[:, :], ps_d[:, :], ALU.mult).then_inc(o_out, 1)

                def slot(b, u):
                    if u % 4 == 0 and live_group(b, (u - 8) // 4):
                        cap(b, (u - 8) // 4)
                    if live(b, u):
                        negated(b, u)
                    if live(b, u - 1):
                        parts(b, u - 1)
                    if u % 4 == 1 and live_group(b, (u - 9) // 4):
                        heads_out(b, (u - 9) // 4)
                    if u == 11 and live(b, u):
                        group_wait(dve, k_proj, b, 3)
                        after = (b + 1) & 3
                        dve.tensor_copy(x[:, :], XT[:, after, 1:1 + N]).then_inc(x_in, 1)

                over_slots(dve, slot)

            @block.gpsimd
            def _(pool):
                pool.wait_ge(set_up, 3)

                def mask(b, u):
                    unit_wait(pool, zd, b, u, 4)
                    pool.tensor_tensor(tick[:, u:u + 1], dist[:, 0:1], dist[:, 0:1], ALU.mult)
                    view = z[:, u % 4, :, 0:P]
                    pool.affine_select(out=view, in_=view, compare_op=ALU.is_ge, fill=10000.0, base=0,
                                       pattern=[[0, 4], [1, P]], channel_multiplier=-1).then_inc(masked, 1)

                def subtract(b, u):
                    n, ring = N - P * (u % 4), u % 4
                    unit_wait(pool, lned, b, u)
                    pool.tensor_tensor(z[:, ring, :, 0:n], a[:, ring, :, 0:n], z[:, ring, :, 0:n], ALU.subtract).then_inc(subd, 1)

                def slot(b, u):
                    if live(b, u):
                        mask(b, u)
                    if live(b, u - 2):
                        subtract(b, u - 2)

                over_slots(pool, slot)


def swiglu(nc, w, XT, YT):
    chunks = HIDDEN // P
    with ExitStack() as ctx:
        sb = lambda name, shape, dt=F32: ctx.enter_context(nc.sbuf_tensor("sg_" + name, shape, dt))
        ps = lambda name, shape, dt=F32: ctx.enter_context(nc.psum_tensor("sg_" + name, shape, dt))
        sem = lambda name: ctx.enter_context(nc.semaphore("sg_" + name))
        raw = sb("raw", [P, 3, HIDDEN], I32)
        wf = sb("wf", [P, 3, HIDDEN])
        act_g = sb("act_g", [P, chunks, N])
        h = sb("h", [P, chunks, N])
        ps_g, ps_u, ps_y = ps("ps_g", [P, chunks, N]), ps("ps_u", [P, chunks, N]), ps("ps_y", [P, N])
        loaded, dequant, gated, upped, silued, hid, downed, y_out = (
            sem(n) for n in ("loaded", "dequant", "gated", "upped", "silued", "hid", "downed", "y_out"))

        with nc.Block() as block:

            @block.sync
            def _(sp):
                for k, key in enumerate(("sg_gate", "sg_up", "sg_down")):
                    sp.dma_start(raw[:, k, :], w[key]).then_inc(loaded, 16)

            @block.tensor
            def _(pe):
                pe.wait_ge(dequant, 1)

                def work(b):
                    for c in range(chunks):
                        for k, (bank, done, used, n_used) in enumerate(((ps_g, gated, silued, 1), (ps_u, upped, hid, 1))):
                            if not isinstance(b, int):
                                pe.wait_ge(used, b * chunks + (c + 1 - chunks))
                            pe.matmul(bank[:, c, :], wf[:, k, P * c:P * c + P], XT[:, b, 1:1 + N],
                                      start=True, stop=True).then_inc(done, 1)
                    if not isinstance(b, int):
                        pe.wait_ge(y_out, b)
                    for c in range(chunks):
                        pe.wait_ge(hid, b * chunks + (c + 1))
                        mm = pe.matmul(ps_y[:, :], wf[:, 2, P * c:P * c + P], h[:, c, :], start=(c == 0), stop=(c == chunks - 1))
                    mm.then_inc(downed, 1)

                over_elements(pe, work)

            @block.scalar
            def _(act):
                def work(b):
                    for c in range(chunks):
                        act.wait_ge(gated, b * chunks + (c + 1))
                        act.activation(act_g[:, c, :], ps_g[:, c, :], ACT.Silu).then_inc(silued, 1)
                    act.wait_ge(downed, b + 1)
                    act.activation(YT[:, b, 1:1 + N], ps_y[:, :], ACT.Copy).then_inc(y_out, 1)

                over_elements(act, work)

            @block.vector
            def _(dve):
                dve.wait_ge(loaded, 48)
                dve.tensor_scalar(wf[:, :, :], raw[:, :, :], float(np.float32(1.0 / 127.0)), None, ALU.mult).then_inc(dequant, 1)

                def work(b):
                    for c in range(chunks):
                        dve.wait_ge(silued, b * chunks + (c + 1))
                        dve.wait_ge(upped, b * chunks + (c + 1))
                        if c == 0 and not isinstance(b, int):
                            dve.wait_ge(downed, b)
                        dve.tensor_tensor(h[:, c, :], act_g[:, c, :], ps_u[:, c, :], ALU.mult).then_inc(hid, 1)

                over_elements(dve, work)


def build(nc, a, out):
    with ExitStack() as ctx:
        sb = lambda name, shape, dt=F32: ctx.enter_context(nc.sbuf_tensor(name, shape, dt))
        X = sb("X", [P, B, 4, DIM])
        XT = sb("XT", [P, B, N + 2])
        ident = sb("ident", [P, P])
        iload = ctx.enter_context(nc.semaphore("iload"))
        with nc.Block() as block:
            @block.sync
            def _(sp):
                sp.dma_start(ident[:, :], a["ident"]).then_inc(iload, 16)
                sp.wait_ge(iload, 16)
        sems = {name: ctx.enter_context(nc.semaphore("ln_" + name)) for name in (
            "loaded", "y_turned", "stat", "aggr", "lned", "rstd", "centred", "scaled", "added", "x_turned", "stored",
            "eps_set", "xt_out")}
        before = dict.fromkeys(sems, 0)
        tok = lambda d: d.rearrange("b (k p) c -> b p k c", p=P)
        add_and_normalise(nc, "_0", sems, before, ident, X, None, XT, x_dram=tok(a["x"]))
        with nc.sbuf_tensor("YT_a", [P, B, N + 2], F32) as YT:
            linear_attention(nc, a, XT, YT)
            add_and_normalise(nc, "_1", sems, before, ident, X, YT, XT)
        windowed_attention_stack(nc, a, XT)
        with nc.sbuf_tensor("YT_b", [P, B, N + 2], F32) as YT:
            add_and_normalise(nc, "_2", sems, before, ident, X, XT, YT)
            power_attention(nc, a, YT, XT)
            add_and_normalise(nc, "_3", sems, before, ident, X, XT, YT)
            swiglu(nc, a, YT, XT)
            add_and_normalise(nc, "_4", sems, before, ident, X, XT, None, out_dram=tok(out))


def rotary():
    f = np.float32
    half = np.arange(0, 64, 2, dtype=f)
    t = np.arange(N, dtype=f)
    freqs = t[:, None] * (f(1.0) / f(10000.0) ** (half / f(64)))[None, :]
    base = (half + f(0.4 * 64)) / f(1.4 * 64)
    scale = base[None, :] ** ((t - N // 2) / f(W // 2))[:, None]
    def lay(table):
        q, k = table * scale * f(8 * 65536), table * (f(1.0) / scale) * f(65536)
        return np.ascontiguousarray(np.tile(np.stack([q.T, k.T], 1), (4, 1, 1)).astype(f))
    return lay(np.cos(freqs)), lay(np.sin(freqs))


def constants():
    i = np.arange(P)
    f = np.float32
    q, key = np.meshgrid(i % W, np.arange(2 * W), indexing="ij")
    ok = (q <= key) & (key <= q + W)
    first = ok & ~((i[:, None] < W) & (key < W))
    m = np.stack([first, first, *[ok] * 6], 1)
    cos, sin = rotary()
    return {
        "ident": np.eye(P, dtype=f),
        "ident16": np.eye(P).astype(mybir.dt.np(BF16)),
        "head_ones": (i[:, None] // W == i[None, :] // W).astype(f),
        "mean_ones": np.full((P, P), 1.0 / DIM, f),
        "mask16": np.where(m, 0.0, BIG).reshape(P, N).astype(mybir.dt.np(BF16)),
        "la_blocks": (i[:, None] // 8 == i[None, :] // 8).astype(f),
        "pa_dist": (np.arange(N)[None, :] - i[:, None]).astype(f),
        "pa_row8": ((i[:, None] % 32 == 8) & (i[None, :] % 32 < 8) & (i[:, None] // 32 == i[None, :] // 32)).astype(f),
        "cos_t": cos, "sin_t": sin,
    }


def lay_out(inp):
    f = lambda k: np.asarray(inp[k])
    Wqkv = f("L0_ffn_Wqkv")
    halves = lambda m: m.reshape(DEPTH, DIM, 4, 4, 2, 32).transpose(0, 2, 1, 4, 3, 5).reshape(DEPTH, 4, DIM, 256)
    v = Wqkv[:, :, 2048:].reshape(DEPTH, DIM, 4, 256).transpose(0, 2, 1, 3)
    gains = lambda m: np.tile(m.reshape(DEPTH, 2, 32).transpose(0, 2, 1), (1, 4, 1))
    pad = lambda m, n: np.concatenate([m, np.zeros((m.shape[0], n - m.shape[1], *m.shape[2:]), m.dtype)], 1)
    b1 = f("L0_ffn_b1").reshape(DEPTH, 2, INNER2).transpose(0, 2, 1)
    b1 = pad(b1, 3 * P).reshape(DEPTH, 3, P, 2).transpose(0, 2, 3, 1).reshape(DEPTH, P, 6)
    col = lambda k: f(k)[..., None]
    return {
        "x": f("L0_attn_x"),
        "la_wq": f("L0_attn_Wq").T,
        "la_wkv": np.concatenate([f("L0_attn_Wk").T, f("L0_attn_Wv").T], 1),
        "la_wp": f("L0_attn_Wp").T,
        "la_vec": np.concatenate([f("L0_attn_conv_w"), col("L0_attn_conv_b"), col("L0_attn_bp")], 1),
        "w_qkv": np.concatenate([halves(Wqkv[:, :, :1024]), halves(Wqkv[:, :, 1024:2048]), v], 3),
        "w_o": f("L0_ffn_Wo").reshape(DEPTH, 8, P, DIM).transpose(0, 2, 1, 3),
        "w_up": f("L0_ffn_W1"),
        "w_down": pad(f("L0_ffn_W2"), 3 * P).reshape(DEPTH, 3, P, DIM).transpose(0, 2, 1, 3),
        "qk_gain": np.concatenate([gains(f("L0_ffn_q_scale")), gains(f("L0_ffn_k_scale"))], 2),
        "ffn_vec": np.concatenate([col("L0_ffn_ln_g"), col("L0_ffn_ln_b"), b1, col("L0_ffn_b2")], 2),
        "pa_wq": f("L1_attn_Wq").T, "pa_wk": f("L1_attn_Wk").T, "pa_wv": f("L1_attn_Wv").T, "pa_wo": f("L1_attn_Wo").T,
        "pa_slopes": np.tile(f("L1_attn_alibi_slopes")[None], (P, 1)),
        "pa_power": np.tile(f("L1_attn_power")[None], (P, 1)),
        "sg_gate": f("L1_ffn_w_gate").T, "sg_up": f("L1_ffn_w_up").T,
        "sg_down": f("L1_ffn_w_down").T.reshape(HIDDEN // P, P, DIM).transpose(1, 0, 2).reshape(P, HIDDEN),
    }


def kernel(**inputs):
    import concourse.bacc as bacc
    from concourse.bass_utils import run_bass_kernel_spmd as launch
    nc = bacc.Bacc("TRN2", target_bir_lowering=False, num_devices=1)
    arrays = {**lay_out(inputs), **constants()}
    arrays = {k: np.ascontiguousarray(v) for k, v in arrays.items()}
    aps = {k: nc.dram_tensor("in_" + k, v.shape, mybir.dt.from_np(v.dtype), kind="ExternalInput").ap()
           for k, v in arrays.items()}
    out = nc.dram_tensor("out_0", (B, N, DIM), F32, kind="ExternalOutput").ap()
    build(nc, aps, out)
    r = launch(nc, [{"in_" + k: v for k, v in arrays.items()}], core_ids=[0])
    return r.results[0]["out_0"]
```
